# Optimizing a Trainium2 kernel written in Bass

```python
import numpy as np
import jax
import jax.numpy as jnp

def _softmax(x, axis=-1):
    return jax.nn.softmax(x, axis=axis)

def _gelu(x):
    return jax.nn.gelu(x, approximate=True)

def _silu(x):
    return jax.nn.silu(x)

def _sigmoid(x):
    return jax.nn.sigmoid(x)

def _layernorm(x, axis=-1, eps=1e-05):
    m = jnp.mean(x, axis=axis, keepdims=True)
    v = jnp.var(x, axis=axis, keepdims=True)
    return (x - m) / jnp.sqrt(v + eps)

def _scatter_add(tgt, idx, src, axis=0):
    return tgt.at[idx].add(src)

def _segment_sum(src, seg, n):
    return jax.ops.segment_sum(src, seg, n)
kernel_name = 'mk_vit_tower_d2_tok_img768_r4_23af67'

def setup_inputs(seed: int=0):
    np.random.seed(seed)
    _w = jnp.asarray

    def _rec_inputs():
        import jax
        import jax.numpy as jnp
        _rk = jax.random.key(seed)
        x = -0.00016672 + 0.999947 * jax.random.normal(jax.random.fold_in(_rk, 1), (32, 3, 112, 112), jnp.float32)
        return x
    x = _rec_inputs()

    def _L0_tok_setup():
        import jax, jax.numpy as jnp
        import numpy as np
        IMAGE_SIZE = 96
        PATCH = 16
        EMBED_DIM = 192
        IN_DIM = PATCH * PATCH * 3
        key = jax.random.key(seed)
        kx, kw = jax.random.split(key)
        x = jax.random.normal(kx, (64, 3, IMAGE_SIZE, IMAGE_SIZE), dtype=jnp.float32)
        W = jax.random.normal(kw, (EMBED_DIM, IN_DIM), dtype=jnp.float32) * (1.0 / np.sqrt(IN_DIM))
        return {'x': x, 'W': W}
    _L0_tok_all = _L0_tok_setup()
    _L0_tok_in = {k: v for k, v in _L0_tok_all.items() if k in ('W',)}
    del _L0_tok_all

    def _L0_attn_setup():
        import jax, jax.numpy as jnp
        import numpy as np
        D_MODEL = 192
        D_STATE = 16
        D_CONV = 4
        EXPAND = 2
        D_INNER = EXPAND * D_MODEL
        DT_RANK = (D_MODEL + 15) // 16
        BATCH = 4
        SEQ = 512

        def _mamba(x, W_in, conv_w, conv_b, W_x, W_dt, b_dt, A_log, D, W_out):
            B_, L, _ = x.shape
            K = conv_w.shape[1]
            xz = jnp.einsum('bld,ed->ble', x, W_in)
            xc, z = jnp.split(xz, 2, axis=-1)
            xp = jnp.pad(xc, ((0, 0), (K - 1, 0), (0, 0)))
            xconv = conv_b + sum((conv_w[:, k] * xp[:, k:k + L, :] for k in range(K)))
            xconv = jax.nn.silu(xconv)
            proj = jnp.einsum('bld,ed->ble', xconv, W_x)
            dtr = proj[..., :DT_RANK]
            Bt = proj[..., DT_RANK:DT_RANK + D_STATE]
            Ct = proj[..., DT_RANK + D_STATE:]
            dt = jax.nn.softplus(jnp.einsum('blr,dr->bld', dtr, W_dt) + b_dt)
            A = -jnp.exp(A_log)

            def step(h, inp):
                u, d, b, c = inp
                dA = jnp.exp(d[..., None] * A)
                h = dA * h + (d * u)[..., None] * b[:, None, :]
                y = jnp.einsum('bdn,bn->bd', h, c)
                return (h, y)
            h0 = jnp.zeros((B_, D_INNER, D_STATE), x.dtype)
            xs = (xconv.transpose(1, 0, 2), dt.transpose(1, 0, 2), Bt.transpose(1, 0, 2), Ct.transpose(1, 0, 2))
            _, ys = jax.lax.scan(step, h0, xs)
            y = ys.transpose(1, 0, 2) + xconv * D
            y = y * jax.nn.silu(z)
            return jnp.einsum('bld,ed->ble', y, W_out)
        key = jax.random.key(seed)
        ks = jax.random.split(key, 20)

        def nrm(k, shape, scale=0.02):
            return (jax.random.normal(k, shape) * scale).astype(jnp.float32)
        inp = {'x': jax.random.normal(ks[0], (BATCH, SEQ, D_MODEL), dtype=jnp.float32)}
        i = 1
        for p in ('fwd', 'bwd'):
            inp[p + '_W_in'] = nrm(ks[i], (2 * D_INNER, D_MODEL))
            i += 1
            inp[p + '_conv_w'] = nrm(ks[i], (D_INNER, D_CONV), 0.2)
            i += 1
            inp[p + '_conv_b'] = jnp.zeros((D_INNER,), jnp.float32)
            inp[p + '_W_x'] = nrm(ks[i], (DT_RANK + 2 * D_STATE, D_INNER))
            i += 1
            inp[p + '_W_dt'] = nrm(ks[i], (D_INNER, DT_RANK), 0.1)
            i += 1
            inp[p + '_b_dt'] = nrm(ks[i], (D_INNER,), 0.5)
            i += 1
            inp[p + '_A_log'] = jnp.tile(jnp.log(jnp.arange(1, D_STATE + 1, dtype=jnp.float32)), (D_INNER, 1))
            inp[p + '_D'] = jnp.ones((D_INNER,), jnp.float32)
            inp[p + '_W_out'] = nrm(ks[i], (D_MODEL, D_INNER))
            i += 1
        inp['ln_g'] = jnp.ones((D_MODEL,), jnp.float32)
        inp['ln_b'] = jnp.zeros((D_MODEL,), jnp.float32)
        return inp
    _L0_attn_all = _L0_attn_setup()
    _L0_attn_in = {k: v for k, v in _L0_attn_all.items() if k in ('fwd_W_in', 'fwd_conv_w', 'fwd_conv_b', 'fwd_W_x', 'fwd_W_dt', 'fwd_b_dt', 'fwd_A_log', 'fwd_D', 'fwd_W_out', 'bwd_W_in', 'bwd_conv_w', 'bwd_conv_b', 'bwd_W_x', 'bwd_W_dt', 'bwd_b_dt', 'bwd_A_log', 'bwd_D', 'bwd_W_out', 'ln_g', 'ln_b')}
    del _L0_attn_all

    def _L0_ffn_setup():
        import jax, jax.numpy as jnp
        import numpy as np
        B, M, D = (32, 196, 192)
        N, P, H = (64, 1, 768)
        EPS = 1e-12

        def _l2norm(v, axis):
            n = jnp.sqrt(jnp.sum(v * v, axis=axis, keepdims=True))
            return v / jnp.maximum(n, EPS)
        key = jax.random.key(seed)
        ks = jax.random.split(key, 7)
        x = jax.random.normal(ks[0], (B, M, D), dtype=jnp.float32)
        phi = jax.random.normal(ks[1], (D, N, P), dtype=jnp.float32) * (1.0 / D ** 0.5)
        scale = jnp.ones((1,), dtype=jnp.float32)
        w1 = jax.random.normal(ks[2], (N, D, H), dtype=jnp.float32) * (1.0 / D ** 0.5)
        b1 = jnp.zeros((N, H), dtype=jnp.float32)
        w2 = jax.random.normal(ks[3], (N, H, D), dtype=jnp.float32) * (1.0 / H ** 0.5)
        b2 = jnp.zeros((N, D), dtype=jnp.float32)
        return {'x': x, 'phi': phi, 'scale': scale, 'w1': w1, 'b1': b1, 'w2': w2, 'b2': b2}
    _L0_ffn_all = _L0_ffn_setup()
    _L0_ffn_in = {k: v for k, v in _L0_ffn_all.items() if k in ('phi', 'scale', 'w1', 'b1', 'w2', 'b2')}
    del _L0_ffn_all

    def _L1_attn_setup():
        import jax, jax.numpy as jnp
        import numpy as np
        EPS = 1e-05
        B, T, C = (8, 512, 192)
        H = 4 * C
        LAYER_ID, N_LAYER = (4, 12)

        def _ln(x, w, b):
            mu = x.mean(-1, keepdims=True)
            var = ((x - mu) ** 2).mean(-1, keepdims=True)
            return (x - mu) / jnp.sqrt(var + EPS) * w + b

        def _wkv_scan(w, k, v):
            a0 = jnp.zeros(k.shape[1:], k.dtype)
            b0 = jnp.zeros_like(a0)
            m0 = jnp.full_like(a0, -1e+38)

            def step(carry, kv):
                a, b, m = carry
                kt, vt = kv
                mm = jnp.maximum(m + w, kt)
                e1 = jnp.exp(m + w - mm)
                e2 = jnp.exp(kt - mm)
                return ((e1 * a + e2 * vt, e1 * b + e2, mm), (a, b, m))
            _, (A, Bd, M) = jax.lax.scan(step, (a0, b0, m0), (k, v))
            return (A, Bd, M)

        def bi_wkv(w, u, k, v):
            kt = jnp.swapaxes(k, 0, 1)
            vt = jnp.swapaxes(v, 0, 1)
            af, bf, mf = _wkv_scan(w, kt, vt)
            ab, bb, mb = _wkv_scan(w, kt[::-1], vt[::-1])
            ab, bb, mb = (ab[::-1], bb[::-1], mb[::-1])
            kk = kt + u
            M = jnp.maximum(jnp.maximum(mf, mb), kk)
            ef = jnp.exp(mf - M)
            eb = jnp.exp(mb - M)
            ec = jnp.exp(kk - M)
            y = (ef * af + eb * ab + ec * vt) / (ef * bf + eb * bb + ec)
            return jnp.swapaxes(y, 0, 1)
        key = jax.random.key(seed)
        ks = jax.random.split(key, 9)
        x = jax.random.normal(ks[0], (B, T, C), jnp.float32)
        r01 = LAYER_ID / (N_LAYER - 1)
        h = np.arange(C, dtype=np.float64)
        decay = (-5.0 + 8.0 * (h / (C - 1)) ** (0.7 + 1.3 * r01)).astype(np.float32)
        zigzag = ((np.arange(C) + 1) % 3 - 1).astype(np.float32) * 0.5
        first = (np.float32(np.log(0.3)) + zigzag).astype(np.float32)
        s = 0.02
        return {'x': x, 'ln1_w': jnp.ones((C,), jnp.float32), 'ln1_b': jnp.zeros((C,), jnp.float32), 'ln2_w': jnp.ones((C,), jnp.float32), 'ln2_b': jnp.zeros((C,), jnp.float32), 'decay': jnp.asarray(decay), 'first': jnp.asarray(first), 'Wk_a': s * jax.random.normal(ks[1], (C, C), jnp.float32), 'Wv_a': s * jax.random.normal(ks[2], (C, C), jnp.float32), 'Wr_a': s * jax.random.normal(ks[3], (C, C), jnp.float32), 'Wo_a': s * jax.random.normal(ks[4], (C, C), jnp.float32), 'Wk_f': s * jax.random.normal(ks[5], (H, C), jnp.float32), 'Wv_f': s * jax.random.normal(ks[6], (C, H), jnp.float32), 'Wr_f': s * jax.random.normal(ks[7], (C, C), jnp.float32)}
    _L1_attn_all = _L1_attn_setup()
    _L1_attn_in = {k: v for k, v in _L1_attn_all.items() if k in ('ln1_w', 'ln1_b', 'ln2_w', 'ln2_b', 'decay', 'first', 'Wk_a', 'Wv_a', 'Wr_a', 'Wo_a', 'Wk_f', 'Wv_f', 'Wr_f')}
    del _L1_attn_all

    def _L1_ffn_setup():
        import jax, jax.numpy as jnp
        import numpy as np
        E = 192
        H = 12
        D = E // H
        HID = 768
        NEXP = 4
        TOPK = 2
        EPS = 1e-05

        def _ln(x, g, b):
            m = jnp.mean(x, axis=-1, keepdims=True)
            v = jnp.mean(jnp.square(x - m), axis=-1, keepdims=True)
            return (x - m) * jax.lax.rsqrt(v + EPS) * g + b
        key = jax.random.key(seed)
        ks = jax.random.split(key, 10)
        s = 0.02
        return {'x': jax.random.normal(ks[0], (8, 256, E), jnp.float32), 'ln1_g': jnp.ones((E,), jnp.float32), 'ln1_b': jnp.zeros((E,), jnp.float32), 'in_w': jax.random.normal(ks[1], (3 * E, E), jnp.float32) * s, 'in_b': jnp.zeros((3 * E,), jnp.float32), 'out_w': jax.random.normal(ks[2], (E, E), jnp.float32) * s, 'out_b': jnp.zeros((E,), jnp.float32), 'mlp_w1': jax.random.normal(ks[3], (E, HID), jnp.float32) * s, 'mlp_b1': jnp.zeros((HID,), jnp.float32), 'mlp_w2': jax.random.normal(ks[4], (HID, E), jnp.float32) * s, 'mlp_b2': jnp.zeros((E,), jnp.float32), 'ln2_g': jnp.ones((E,), jnp.float32), 'ln2_b': jnp.zeros((E,), jnp.float32), 'gate_w': jax.random.normal(ks[5], (NEXP, E), jnp.float32) * s, 'gate_b': jnp.zeros((NEXP,), jnp.float32), 'exp_w1': jax.random.normal(ks[6], (NEXP, E, HID), jnp.float32) * s, 'exp_b1': jnp.zeros((NEXP, HID), jnp.float32), 'exp_w2': jax.random.normal(ks[7], (NEXP, HID, E), jnp.float32) * s, 'exp_b2': jnp.zeros((NEXP, E), jnp.float32)}
    _L1_ffn_all = _L1_ffn_setup()
    _L1_ffn_in = {k: v for k, v in _L1_ffn_all.items() if k in ('ln1_g', 'ln1_b', 'in_w', 'in_b', 'out_w', 'out_b', 'mlp_w1', 'mlp_b1', 'mlp_w2', 'mlp_b2', 'ln2_g', 'ln2_b', 'gate_w', 'gate_b', 'exp_w1', 'exp_b1', 'exp_w2', 'exp_b2')}
    del _L1_ffn_all
    return {'x': x, 'L0_tok_W': _L0_tok_in['W'], 'L0_attn_fwd_W_in': _L0_attn_in['fwd_W_in'], 'L0_attn_fwd_conv_w': _L0_attn_in['fwd_conv_w'], 'L0_attn_fwd_conv_b': _L0_attn_in['fwd_conv_b'], 'L0_attn_fwd_W_x': _L0_attn_in['fwd_W_x'], 'L0_attn_fwd_W_dt': _L0_attn_in['fwd_W_dt'], 'L0_attn_fwd_b_dt': _L0_attn_in['fwd_b_dt'], 'L0_attn_fwd_A_log': _L0_attn_in['fwd_A_log'], 'L0_attn_fwd_D': _L0_attn_in['fwd_D'], 'L0_attn_fwd_W_out': _L0_attn_in['fwd_W_out'], 'L0_attn_bwd_W_in': _L0_attn_in['bwd_W_in'], 'L0_attn_bwd_conv_w': _L0_attn_in['bwd_conv_w'], 'L0_attn_bwd_conv_b': _L0_attn_in['bwd_conv_b'], 'L0_attn_bwd_W_x': _L0_attn_in['bwd_W_x'], 'L0_attn_bwd_W_dt': _L0_attn_in['bwd_W_dt'], 'L0_attn_bwd_b_dt': _L0_attn_in['bwd_b_dt'], 'L0_attn_bwd_A_log': _L0_attn_in['bwd_A_log'], 'L0_attn_bwd_D': _L0_attn_in['bwd_D'], 'L0_attn_bwd_W_out': _L0_attn_in['bwd_W_out'], 'L0_attn_ln_g': _L0_attn_in['ln_g'], 'L0_attn_ln_b': _L0_attn_in['ln_b'], 'L0_ffn_phi': _L0_ffn_in['phi'], 'L0_ffn_scale': _L0_ffn_in['scale'], 'L0_ffn_w1': _L0_ffn_in['w1'], 'L0_ffn_b1': _L0_ffn_in['b1'], 'L0_ffn_w2': _L0_ffn_in['w2'], 'L0_ffn_b2': _L0_ffn_in['b2'], 'L1_attn_ln1_w': _L1_attn_in['ln1_w'], 'L1_attn_ln1_b': _L1_attn_in['ln1_b'], 'L1_attn_ln2_w': _L1_attn_in['ln2_w'], 'L1_attn_ln2_b': _L1_attn_in['ln2_b'], 'L1_attn_decay': _L1_attn_in['decay'], 'L1_attn_first': _L1_attn_in['first'], 'L1_attn_Wk_a': _L1_attn_in['Wk_a'], 'L1_attn_Wv_a': _L1_attn_in['Wv_a'], 'L1_attn_Wr_a': _L1_attn_in['Wr_a'], 'L1_attn_Wo_a': _L1_attn_in['Wo_a'], 'L1_attn_Wk_f': _L1_attn_in['Wk_f'], 'L1_attn_Wv_f': _L1_attn_in['Wv_f'], 'L1_attn_Wr_f': _L1_attn_in['Wr_f'], 'L1_ffn_ln1_g': _L1_ffn_in['ln1_g'], 'L1_ffn_ln1_b': _L1_ffn_in['ln1_b'], 'L1_ffn_in_w': _L1_ffn_in['in_w'], 'L1_ffn_in_b': _L1_ffn_in['in_b'], 'L1_ffn_out_w': _L1_ffn_in['out_w'], 'L1_ffn_out_b': _L1_ffn_in['out_b'], 'L1_ffn_mlp_w1': _L1_ffn_in['mlp_w1'], 'L1_ffn_mlp_b1': _L1_ffn_in['mlp_b1'], 'L1_ffn_mlp_w2': _L1_ffn_in['mlp_w2'], 'L1_ffn_mlp_b2': _L1_ffn_in['mlp_b2'], 'L1_ffn_ln2_g': _L1_ffn_in['ln2_g'], 'L1_ffn_ln2_b': _L1_ffn_in['ln2_b'], 'L1_ffn_gate_w': _L1_ffn_in['gate_w'], 'L1_ffn_gate_b': _L1_ffn_in['gate_b'], 'L1_ffn_exp_w1': _L1_ffn_in['exp_w1'], 'L1_ffn_exp_b1': _L1_ffn_in['exp_b1'], 'L1_ffn_exp_w2': _L1_ffn_in['exp_w2'], 'L1_ffn_exp_b2': _L1_ffn_in['exp_b2']}

def reference(x, L0_tok_W, L0_attn_fwd_W_in, L0_attn_fwd_conv_w, L0_attn_fwd_conv_b, L0_attn_fwd_W_x, L0_attn_fwd_W_dt, L0_attn_fwd_b_dt, L0_attn_fwd_A_log, L0_attn_fwd_D, L0_attn_fwd_W_out, L0_attn_bwd_W_in, L0_attn_bwd_conv_w, L0_attn_bwd_conv_b, L0_attn_bwd_W_x, L0_attn_bwd_W_dt, L0_attn_bwd_b_dt, L0_attn_bwd_A_log, L0_attn_bwd_D, L0_attn_bwd_W_out, L0_attn_ln_g, L0_attn_ln_b, L0_ffn_phi, L0_ffn_scale, L0_ffn_w1, L0_ffn_b1, L0_ffn_w2, L0_ffn_b2, L1_attn_ln1_w, L1_attn_ln1_b, L1_attn_ln2_w, L1_attn_ln2_b, L1_attn_decay, L1_attn_first, L1_attn_Wk_a, L1_attn_Wv_a, L1_attn_Wr_a, L1_attn_Wo_a, L1_attn_Wk_f, L1_attn_Wv_f, L1_attn_Wr_f, L1_ffn_ln1_g, L1_ffn_ln1_b, L1_ffn_in_w, L1_ffn_in_b, L1_ffn_out_w, L1_ffn_out_b, L1_ffn_mlp_w1, L1_ffn_mlp_b1, L1_ffn_mlp_w2, L1_ffn_mlp_b2, L1_ffn_ln2_g, L1_ffn_ln2_b, L1_ffn_gate_w, L1_ffn_gate_b, L1_ffn_exp_w1, L1_ffn_exp_b1, L1_ffn_exp_w2, L1_ffn_exp_b2):
    import jax
    import jax.numpy as jnp

    def _L0_tok_ref(x, W):
        import jax, jax.numpy as jnp
        import numpy as np
        IMAGE_SIZE = 96
        PATCH = 16
        EMBED_DIM = 192
        IN_DIM = PATCH * PATCH * 3
        b, c, h, w = x.shape
        ph = pw = PATCH
        gh, gw = (h // ph, w // pw)
        patches = x.reshape(b, c, gh, ph, gw, pw)
        patches = patches.transpose(0, 2, 4, 1, 3, 5)
        patches = patches.reshape(b, gh * gw, c * ph * pw)
        return jnp.einsum('bnd,ed->bne', patches, W)

    def _L0_attn_ref(x, fwd_W_in, fwd_conv_w, fwd_conv_b, fwd_W_x, fwd_W_dt, fwd_b_dt, fwd_A_log, fwd_D, fwd_W_out, bwd_W_in, bwd_conv_w, bwd_conv_b, bwd_W_x, bwd_W_dt, bwd_b_dt, bwd_A_log, bwd_D, bwd_W_out, ln_g, ln_b):
        import jax, jax.numpy as jnp
        import numpy as np
        D_MODEL = 192
        D_STATE = 16
        D_CONV = 4
        EXPAND = 2
        D_INNER = EXPAND * D_MODEL
        DT_RANK = (D_MODEL + 15) // 16
        BATCH = 4
        SEQ = 512

        def _mamba(x, W_in, conv_w, conv_b, W_x, W_dt, b_dt, A_log, D, W_out):
            B_, L, _ = x.shape
            K = conv_w.shape[1]
            xz = jnp.einsum('bld,ed->ble', x, W_in)
            xc, z = jnp.split(xz, 2, axis=-1)
            xp = jnp.pad(xc, ((0, 0), (K - 1, 0), (0, 0)))
            xconv = conv_b + sum((conv_w[:, k] * xp[:, k:k + L, :] for k in range(K)))
            xconv = jax.nn.silu(xconv)
            proj = jnp.einsum('bld,ed->ble', xconv, W_x)
            dtr = proj[..., :DT_RANK]
            Bt = proj[..., DT_RANK:DT_RANK + D_STATE]
            Ct = proj[..., DT_RANK + D_STATE:]
            dt = jax.nn.softplus(jnp.einsum('blr,dr->bld', dtr, W_dt) + b_dt)
            A = -jnp.exp(A_log)

            def step(h, inp):
                u, d, b, c = inp
                dA = jnp.exp(d[..., None] * A)
                h = dA * h + (d * u)[..., None] * b[:, None, :]
                y = jnp.einsum('bdn,bn->bd', h, c)
                return (h, y)
            h0 = jnp.zeros((B_, D_INNER, D_STATE), x.dtype)
            xs = (xconv.transpose(1, 0, 2), dt.transpose(1, 0, 2), Bt.transpose(1, 0, 2), Ct.transpose(1, 0, 2))
            _, ys = jax.lax.scan(step, h0, xs)
            y = ys.transpose(1, 0, 2) + xconv * D
            y = y * jax.nn.silu(z)
            return jnp.einsum('bld,ed->ble', y, W_out)
        out_fwd = _mamba(x, fwd_W_in, fwd_conv_w, fwd_conv_b, fwd_W_x, fwd_W_dt, fwd_b_dt, fwd_A_log, fwd_D, fwd_W_out)
        out_bwd = jnp.flip(_mamba(jnp.flip(x, 1), bwd_W_in, bwd_conv_w, bwd_conv_b, bwd_W_x, bwd_W_dt, bwd_b_dt, bwd_A_log, bwd_D, bwd_W_out), 1)
        h = out_fwd + out_bwd + x
        mu = h.mean(-1, keepdims=True)
        var = h.var(-1, keepdims=True)
        return (h - mu) * jax.lax.rsqrt(var + 1e-05) * ln_g + ln_b

    def _L0_ffn_ref(x, phi, scale, w1, b1, w2, b2):
        import jax, jax.numpy as jnp
        import numpy as np
        B, M, D = (32, 196, 192)
        N, P, H = (64, 1, 768)
        EPS = 1e-12

        def _l2norm(v, axis):
            n = jnp.sqrt(jnp.sum(v * v, axis=axis, keepdims=True))
            return v / jnp.maximum(n, EPS)
        xn = _l2norm(x, axis=2)
        phin = scale * _l2norm(phi, axis=0)
        logits = jnp.einsum('bmd,dnp->bmnp', xn, phin)
        d = jax.nn.softmax(logits, axis=1)
        b_, m_, n_, p_ = logits.shape
        c = jax.nn.softmax(logits.reshape(b_, m_, n_ * p_), axis=-1).reshape(b_, m_, n_, p_)
        xs = jnp.einsum('bmd,bmnp->bnpd', xn, d)
        h = jax.nn.gelu(jnp.einsum('bnpd,ndh->bnph', xs, w1) + b1[None, :, None, :], approximate=False)
        ys = jnp.einsum('bnph,nhd->bnpd', h, w2) + b2[None, :, None, :]
        y = jnp.einsum('bnpd,bmnp->bmd', ys, c)
        return y

    def _L1_attn_ref(x, ln1_w, ln1_b, ln2_w, ln2_b, decay, first, Wk_a, Wv_a, Wr_a, Wo_a, Wk_f, Wv_f, Wr_f):
        import jax, jax.numpy as jnp
        import numpy as np
        EPS = 1e-05
        B, T, C = (8, 512, 192)
        H = 4 * C
        LAYER_ID, N_LAYER = (4, 12)

        def _ln(x, w, b):
            mu = x.mean(-1, keepdims=True)
            var = ((x - mu) ** 2).mean(-1, keepdims=True)
            return (x - mu) / jnp.sqrt(var + EPS) * w + b

        def _wkv_scan(w, k, v):
            a0 = jnp.zeros(k.shape[1:], k.dtype)
            b0 = jnp.zeros_like(a0)
            m0 = jnp.full_like(a0, -1e+38)

            def step(carry, kv):
                a, b, m = carry
                kt, vt = kv
                mm = jnp.maximum(m + w, kt)
                e1 = jnp.exp(m + w - mm)
                e2 = jnp.exp(kt - mm)
                return ((e1 * a + e2 * vt, e1 * b + e2, mm), (a, b, m))
            _, (A, Bd, M) = jax.lax.scan(step, (a0, b0, m0), (k, v))
            return (A, Bd, M)

        def bi_wkv(w, u, k, v):
            kt = jnp.swapaxes(k, 0, 1)
            vt = jnp.swapaxes(v, 0, 1)
            af, bf, mf = _wkv_scan(w, kt, vt)
            ab, bb, mb = _wkv_scan(w, kt[::-1], vt[::-1])
            ab, bb, mb = (ab[::-1], bb[::-1], mb[::-1])
            kk = kt + u
            M = jnp.maximum(jnp.maximum(mf, mb), kk)
            ef = jnp.exp(mf - M)
            eb = jnp.exp(mb - M)
            ec = jnp.exp(kk - M)
            y = (ef * af + eb * ab + ec * vt) / (ef * bf + eb * bb + ec)
            return jnp.swapaxes(y, 0, 1)
        Bn, Tn, Cn = x.shape
        h = _ln(x, ln1_w, ln1_b)
        k = h @ Wk_a.T
        v = h @ Wv_a.T
        sr = jax.nn.sigmoid(h @ Wr_a.T)
        y = bi_wkv(decay / Tn, first / Tn, k, v)
        x = x + sr * y @ Wo_a.T
        h = _ln(x, ln2_w, ln2_b)
        kf = jnp.square(jax.nn.relu(h @ Wk_f.T))
        x = x + jax.nn.sigmoid(h @ Wr_f.T) * (kf @ Wv_f.T)
        return x

    def _L1_ffn_ref(x, ln1_g, ln1_b, in_w, in_b, out_w, out_b, mlp_w1, mlp_b1, mlp_w2, mlp_b2, ln2_g, ln2_b, gate_w, gate_b, exp_w1, exp_b1, exp_w2, exp_b2):
        import jax, jax.numpy as jnp
        import numpy as np
        E = 192
        H = 12
        D = E // H
        HID = 768
        NEXP = 4
        TOPK = 2
        EPS = 1e-05

        def _ln(x, g, b):
            m = jnp.mean(x, axis=-1, keepdims=True)
            v = jnp.mean(jnp.square(x - m), axis=-1, keepdims=True)
            return (x - m) * jax.lax.rsqrt(v + EPS) * g + b
        B, N, _ = x.shape
        h = _ln(x, ln1_g, ln1_b)
        qkv = h @ in_w.T + in_b
        q, k, v = jnp.split(qkv, 3, axis=-1)
        q = q.reshape(B, N, H, D)
        k = k.reshape(B, N, H, D)
        v = v.reshape(B, N, H, D)
        scores = jnp.einsum('bqhd,bkhd->bhqk', q, k) / jnp.sqrt(jnp.float32(D))
        attn = jax.nn.softmax(scores, axis=-1)
        ctx = jnp.einsum('bhqk,bkhd->bqhd', attn, v).reshape(B, N, E)
        x = x + ctx @ out_w.T + out_b
        x = x + jax.nn.gelu(x @ mlp_w1 + mlp_b1, approximate=False) @ mlp_w2 + mlp_b2
        xm = _ln(x, ln2_g, ln2_b)
        logits = xm @ gate_w.T + gate_b
        topv, topi = jax.lax.top_k(logits, TOPK)
        gates = jax.nn.softmax(topv, axis=-1)
        onehot = jax.nn.one_hot(topi, NEXP, dtype=x.dtype)
        comb = jnp.einsum('bnk,bnke->bne', gates, onehot)
        moe_out = jnp.zeros_like(x)
        for e in range(NEXP):
            he = jax.nn.gelu(xm @ exp_w1[e] + exp_b1[e], approximate=False)
            oe = he @ exp_w2[e] + exp_b2[e]
            moe_out = moe_out + comb[..., e:e + 1] * oe
        return x + moe_out
    h = _L0_tok_ref(x, L0_tok_W)
    h = h + _L0_attn_ref(_layernorm(h, axis=-1), L0_attn_fwd_W_in, L0_attn_fwd_conv_w, L0_attn_fwd_conv_b, L0_attn_fwd_W_x, L0_attn_fwd_W_dt, L0_attn_fwd_b_dt, L0_attn_fwd_A_log, L0_attn_fwd_D, L0_attn_fwd_W_out, L0_attn_bwd_W_in, L0_attn_bwd_conv_w, L0_attn_bwd_conv_b, L0_attn_bwd_W_x, L0_attn_bwd_W_dt, L0_attn_bwd_b_dt, L0_attn_bwd_A_log, L0_attn_bwd_D, L0_attn_bwd_W_out, L0_attn_ln_g, L0_attn_ln_b)
    h = h + _L0_ffn_ref(_layernorm(h, axis=-1), L0_ffn_phi, L0_ffn_scale, L0_ffn_w1, L0_ffn_b1, L0_ffn_w2, L0_ffn_b2)
    h = h + _L1_attn_ref(_layernorm(h, axis=-1), L1_attn_ln1_w, L1_attn_ln1_b, L1_attn_ln2_w, L1_attn_ln2_b, L1_attn_decay, L1_attn_first, L1_attn_Wk_a, L1_attn_Wv_a, L1_attn_Wr_a, L1_attn_Wo_a, L1_attn_Wk_f, L1_attn_Wv_f, L1_attn_Wr_f)
    h = h + _L1_ffn_ref(_layernorm(h, axis=-1), L1_ffn_ln1_g, L1_ffn_ln1_b, L1_ffn_in_w, L1_ffn_in_b, L1_ffn_out_w, L1_ffn_out_b, L1_ffn_mlp_w1, L1_ffn_mlp_b1, L1_ffn_mlp_w2, L1_ffn_mlp_b2, L1_ffn_ln2_g, L1_ffn_ln2_b, L1_ffn_gate_w, L1_ffn_gate_b, L1_ffn_exp_w1, L1_ffn_exp_b1, L1_ffn_exp_w2, L1_ffn_exp_b2)
    return h

_drawn_inputs = setup_inputs


def setup_inputs(seed=0):
    import zlib

    import numpy as np

    out = dict(_drawn_inputs(seed))
    spreads = {'L0_attn_fwd_conv_b': (0.0, 0.8),
     'L0_attn_fwd_D': (1.0, 0.6),
     'L0_attn_bwd_conv_b': (0.0, 0.8),
     'L0_attn_bwd_D': (1.0, 0.6),
     'L0_attn_ln_g': (1.0, 0.2),
     'L0_attn_ln_b': (0.0, 0.1),
     'L0_ffn_b1': (0.0, 0.8),
     'L0_ffn_b2': (0.0, 0.8),
     'L1_attn_ln1_w': (1.0, 0.6),
     'L1_attn_ln1_b': (0.0, 0.8),
     'L1_attn_ln2_w': (1.0, 0.6),
     'L1_attn_ln2_b': (0.0, 0.8),
     'L1_ffn_ln1_g': (1.0, 0.6),
     'L1_ffn_ln1_b': (0.0, 0.8),
     'L1_ffn_in_b': (0.0, 0.8),
     'L1_ffn_out_b': (0.0, 1.384),
     'L1_ffn_mlp_b1': (0.0, 2.0),
     'L1_ffn_mlp_b2': (0.0, 1.703),
     'L1_ffn_ln2_g': (1.0, 0.6),
     'L1_ffn_ln2_b': (0.0, 0.8),
     'L1_ffn_gate_b': (0.0, 0.8),
     'L1_ffn_exp_b1': (0.0, 0.8),
     'L1_ffn_exp_b2': (0.0, 2.0)}
    factors = {'L0_attn_fwd_W_in': 8.0,
     'L0_attn_fwd_conv_w': 8.0,
     'L0_attn_fwd_W_x': 8.0,
     'L0_attn_fwd_W_dt': 8.0,
     'L0_attn_fwd_b_dt': 8.0,
     'L0_attn_fwd_A_log': 8.0,
     'L0_attn_fwd_W_out': 8.0,
     'L0_attn_bwd_W_in': 8.0,
     'L0_attn_bwd_conv_w': 8.0,
     'L0_attn_bwd_W_x': 8.0,
     'L0_attn_bwd_W_dt': 8.0,
     'L0_attn_bwd_b_dt': 8.0,
     'L0_attn_bwd_A_log': 8.0,
     'L0_attn_bwd_W_out': 8.0,
     'L0_ffn_phi': 8.0,
     'L0_ffn_w1': 8.0,
     'L0_ffn_w2': 8.0,
     'L1_attn_decay': 8.0,
     'L1_attn_first': 40.017,
     'L1_attn_Wk_a': 8.0,
     'L1_attn_Wv_a': 8.0,
     'L1_attn_Wr_a': 8.0,
     'L1_attn_Wo_a': 8.0,
     'L1_attn_Wk_f': 6.409,
     'L1_attn_Wv_f': 5.867,
     'L1_attn_Wr_f': 8.0,
     'L1_ffn_in_w': 8.0,
     'L1_ffn_out_w': 7.335,
     'L1_ffn_mlp_w1': 2.735,
     'L1_ffn_gate_w': 3.526,
     'L1_ffn_exp_w1': 3.847,
     'L1_ffn_exp_w2': 3.573}
    for name, (base, spread) in spreads.items():
        noise = np.random.default_rng([zlib.crc32(name.encode()), seed]).standard_normal(out[name].shape)
        drawn = base * np.exp(spread * noise) if base else spread * noise
        out[name] = jnp.asarray(drawn.astype(out[name].dtype))
    for name, factor in factors.items():
        out[name] = (out[name] * factor).astype(out[name].dtype)
    return out
```

```python
from contextlib import ExitStack

import numpy as np

import concourse.bass as bass
from concourse import mybir

F32 = mybir.dt.float32
BF16 = mybir.dt.bfloat16
I32 = mybir.dt.int32
ALU = mybir.AluOpType
ACT = mybir.ActivationFunctionType
AX = mybir.AxisListType

IMAGES, TOKENS, D = 32, 49, 192
T = IMAGES * TOKENS
TILE = 2 * TOKENS
NT = T // TILE
NQ, TQ = 4, 4
QT = TQ * TILE
CH = D // 2
PATCH_CHUNKS = 6
DI, NS, RANK, TAPS = 384, 16, 12, 4
HALF = T // 2
HI = IMAGES // 2
GROUPS = 6
UNITS = GROUPS * NS
SLOTS = 5
PAD = TOKENS + TAPS - 1
NE, HID = 64, 768
EG = 4
HEADS, HD = 12, 16
PAIR = 64 + TOKENS
NX = 4
HC = HID // 128
LN_EPS = 1e-5
ATANH = (2.00000001, 0.66666322, 0.40024595, 0.27965158, 0.28157778)
RSQRT_MAGIC = float(0x5F3759DF)
MIX_CONST = 9
RW_LOADS = 11


class Stage:

    def __init__(self, filled, taken, after=None):
        self.filled, self.taken, self.after = filled, taken, after
        self.banks, self.takers = [], []
        self.before = []

    def fill(self, pe, i):
        for stage, j in self.before[i]:
            stage.wait_taken(pe, j)

    def counted(self, who=None):
        if self.after is None:
            return 0
        n = len(self.after.takers) if who is None else self.after.takers.count(who)
        return self.after.counted(who) + n

    def wait_filled(self, eng, i):
        eng.wait_ge(self.filled, self.counted() + i + 1)

    def wait_taken(self, eng, i):
        who = self.takers[i]
        eng.wait_ge(self.taken[who], self.counted(who) + self.takers[:i + 1].count(who))


class Steps:

    def __init__(self, eng, done):
        self.eng, self.done, self.n = eng, done, 0

    def step(self, ins):
        ins.then_inc(self.done, 1)
        self.n += 1
        return self.n

    def wait(self):
        if self.n:
            self.eng.wait_ge(self.done, self.n)

    def then(self, ins):
        self.step(ins)
        self.wait()


def build_tower(nc, a, out):
    ctx = ExitStack()
    with ctx:
        def sem(name):
            return ctx.enter_context(nc.semaphore(name))

        def sb(name, shape, dt=F32):
            return ctx.enter_context(nc.sbuf_tensor(name, shape, dt))

        h = sb("h", [TILE, NT, D])
        ident = sb("ident", [128, 128])
        ones = sb("ones", [1, 128])
        two_p = sb("two_p", [128, 1])
        stats = sb("stats", [TILE, 8, 6])
        mv = sb("mv", [TILE, NT, 2])
        rstd = sb("rstd", [TILE, NT])
        lnv = sb("lnv", [TILE, NT])
        lnw = sb("lnw", [TILE, NT])
        sc1 = sb("sc1", [TILE, NT])
        sc2 = sb("sc2", [TILE, NT])
        ARENA = 49400
        arena = sb("arena", [128, ARENA])
        psum = [ctx.enter_context(nc.psum_tensor(f"ps{k}", [128, 1024], F32)) for k in range(4)]

        class Region:

            def __init__(self, at=0):
                self.at = at

            def take(self, parts, shape, dt=F32):
                n = int(np.prod(shape)) // (1 if dt == F32 else 2)
                view = arena[0:parts, self.at:self.at + n]
                self.at += n
                assert self.at <= ARENA, self.at
                if dt != F32:
                    view = view.bitcast(dt)
                if len(shape) == 2:
                    view = view.rearrange("p (a b) -> p a b", b=shape[1])
                elif len(shape) == 3:
                    view = view.rearrange("p (a b c) -> p a b c", b=shape[1], c=shape[2])
                return view

        def bank(k, parts=128, lo=0, hi=512, p0=0):
            return psum[k // 2][p0:parts, (k % 2) * 512 + lo:(k % 2) * 512 + hi]

        def two(k, parts, n, p0=0):
            return psum[k // 2][p0:parts, 0:n]

        R = Region()
        xh = R.take(TILE, [NT, D])
        xhT = R.take(CH, [2, T])
        w_in = R.take(CH, [2, 2 * DI])
        w_x = R.take(128, [3, 108])
        w_dt = R.take(108, [DI])
        w_out = [R.take(128, [3, D]) for _ in range(2)]
        taps = R.take(128, [3, TAPS])
        conv_b, dt_b, d_skip = (R.take(128, [3]) for _ in range(3))
        a_neg = R.take(128, [3 * NS])
        bc = R.take(96, [T], BF16)
        sel = R.take(96, [2 * NS, 128], BF16)
        big = R.at
        xconv, zs, dt, du = (R.take(128, [GROUPS, HALF]) for _ in range(4))
        cb_at = R.at
        c_all = R.take(128, [NS, HALF])
        dA = R.take(128, [2, HALF])
        hbuf = R.take(128, [SLOTS, HALF])
        R2 = Region(big)
        patches = R2.take(128, [PATCH_CHUNKS, T])
        w_tok = R2.take(128, [PATCH_CHUNKS, D])
        R3 = Region(cb_at)
        xc = R3.take(128, [3, IMAGES, PAD])
        R5 = Region(cb_at)
        soft_y, soft_e, soft_r, soft_w = (R5.take(128, [2, T]) for _ in range(4))
        R4 = Region(cb_at + NS * HALF + 2 * HALF)
        assert R5.at <= R4.at
        dtr = R4.take(108, [T])
        res = R4.take(96, [2, QT])
        ln_gb = Region(big)
        g_row = ln_gb.take(TILE, [D])
        b_row = ln_gb.take(TILE, [D])
        hb = ln_gb.take(TILE, [NT, D])
        zln = ln_gb.take(TILE, [NT, D])

        R = Region()
        xn = R.take(TILE, [NT, D])
        xnT = R.take(CH, [2, T])
        phiT = R.take(NE, [D])
        phi_sq = R.take(NE, [D])
        phi_n = R.take(NE, [8])
        phin = R.take(CH, [2, NE])
        scale_b = R.take(NE, [1])
        mask2 = R.take(TILE, [2, NE])
        dlog = R.take(NE, [IMAGES, TOKENS])
        dmax = R.take(NE, [IMAGES])
        dsum = R.take(NE, [IMAGES])
        clog = R.take(TILE, [NT, NE])
        cmax = R.take(TILE, [NT])
        csum = R.take(TILE, [NT])
        dbd = R.take(TILE, [NT, 2 * NE])
        cbd = R.take(TILE, [2, 2 * NE])
        xsT = R.take(CH + 1, [2, NE, IMAGES])
        cT = R.take(128, [NT, TILE])
        ysN = R.take(128, [HI, D])
        hid_e = R.take(128, [2, HID])
        hidT = R.take(128, [2, HC, 128])
        ys = R.take(128, [2, D])
        w1e = R.take(CH + 1, [2, EG * 2, HID])
        w2e = R.take(128, [2, EG * HC, D])
        b2e = R.take(1, [2, EG * D])

        SEG = IMAGES + HI
        W = SEG * TOKENS
        R = Region()
        x1 = R.take(TILE, [NT, D])
        x1_end = R.at
        xa = R.take(TILE, [NT, D])
        xaT = R.take(CH, [2, T])
        w_kvr = R.take(CH, [2, 3 * D])
        w_oA = R.take(128, [D])
        w_oB = R.take(128, [D])
        w_kf = R.take(CH, [2, HID])
        w_vf = R.take(128, [HC, D])
        w_rf = R.take(CH, [2, D])
        aff = R.take(CH, [4, 2])
        wu = R.take(128, [4])
        wu49 = R.take(128, [4])
        kk, vv, sr = (R.take(128, [W]) for _ in range(3))
        step_w = [R.take(128, [W]) for _ in range(2)]
        m_s = [R.take(128, [W + 2]) for _ in range(2)]
        a_s = [R.take(128, [W + 2]) for _ in range(2)]
        b_s = [R.take(128, [W + 2]) for _ in range(2)]
        ex = R.take(128, [9, HALF])
        rw_end = R.at
        R = Region()
        R.at = rw_end - 9 * HALF - 5 * W - 6 * (W + 2)
        kf = R.take(128, [HC, T])
        relu_b = R.take(128, [4, QT])
        sig = R.take(TILE, [NT, D])
        gate = R.take(TILE, [2, D])

        R = Region(x1_end)
        x5two = R.take(CH + 1, [2, 2 * T])
        x5 = R.take(TILE, [NT, D])
        xb_ = R.take(TILE, [NT, D])
        x5T = R.take(CH + 1, [2, T])
        in_w = R.take(CH + 1, [2, 3 * D])
        o_w = R.take(CH + 1, [2, D])
        aff5 = R.take(CH, [4, 2])
        mlp1 = [R.take(CH + 1, [2, HID]) for _ in range(2)]
        mlp2 = [R.take(128, [HC, D]) for _ in range(2)]
        mlp2b = [R.take(TILE, [D]) for _ in range(2)]
        gate_w = R.take(CH + 1, [2, NX])
        top = R.at
        hid = [R.take(128, [HC, T]) for _ in range(2)]
        glog = R.take(TILE, [NT, NX])
        gcmp = R.take(TILE, [NT, NX])
        grank = R.take(TILE, [NT, NX])
        comb = R.take(TILE, [NT, NX])
        gm = R.take(TILE, [NT])
        R = Region(top)
        qT = R.take(CH, [2, T])
        kT = R.take(CH, [2, T])
        kmask = R.take(CH, [6])
        vmask = R.take(TILE, [HEADS, HD])
        kblk = R.take(CH, [8, 6 * TOKENS])
        vblk = R.take(TILE, [8, D])
        prob = R.take(PAIR, [2, HEADS, TOKENS])
        rsum = R.take(PAIR, [2, HEADS])
        smax = R.take(PAIR, [2, HEADS])
        ssum = R.take(PAIR, [2, HEADS])
        probT = R.take(TILE, [4 * 6, PAIR])
        ctxv = R.take(PAIR, [2, D])
        ctxT = R.take(CH + 1, [2, T])

        last_user = [None] * 8

        def stage(name, *engines):
            return Stage(sem(f"{name}_filled"), {e: sem(f"{name}_taken_{e}") for e in engines})

        def use(s, banks, taker):
            prior = [last_user[b] for b in banks if last_user[b] is not None]
            s.before.append(list(dict.fromkeys(prior)))
            s.banks.append(banks)
            s.takers.append(taker)
            for b in banks:
                last_user[b] = (s, len(s.banks) - 1)

        def items(name, n, taker, at=0, of=8, after=None):
            s = stage(name, taker) if after is None else Stage(after.filled, after.taken, after)
            for i in range(n):
                use(s, [at + i % of], taker)
            return s

        s_tok = items("tok", NT, "act")
        s_xhT = items("transp", 8, "act")
        s_xz, s_xp, s_dt, s_wo = [], [], [], []
        for r in range(2):
            s_xz.append(items("xz", 24, "act", after=s_xz[0] if r else None))
            s_xp.append(items("xproj", 4, "dve", after=s_xp[0] if r else None))
            s_dt.append(items("dt", 12, "dve", 4, 4, after=s_dt[0] if r else None))
            for k in range(8):
                last_user[k] = None
            s_wo.append(items("wout", NT, "dve", 6, 2, after=s_wo[0] if r else None))
        NG = NE // EG
        s_phi = items("phiT", 2, "act", 0, 2)
        s_xnT = items("xnT", 8, "act", 2, 6, after=s_xhT)
        s_dl = items("dlogit", 4, "dve", 0, 4)
        s_cl = items("clogit", 2, "dve", 4, 2)
        s_dT = items("dispT", NT, "dve", 0, 4)
        s_cT = items("combT", NT, "act", 4, 2)
        s_xs = items("xsT", 8, "dve", 0, 4)
        s_h1, s_hT, s_y2 = stage("ehid", "act"), stage("ehidT", "dve"), stage("eout", "act")
        for g in range(NG + 2):
            if g < NG:
                for k in range(2):
                    use(s_h1, [(2 * g + k) % 4], "act")
            if 1 <= g <= NG:
                for k in range(2):
                    use(s_hT, [4 + k], "dve")
            if g >= 2:
                use(s_y2, [6 + g % 2], "act")
        s_mix = items("mix", NT, "dve")
        s_xaT = items("xaT", 8, "act", after=s_xnT)
        s_kvr = items("kvr", 18, "act")
        s_wo4 = items("wo4", NT, "dve")
        s_xbT = items("xbT", 8, "act", after=s_xaT)
        s_rf = items("rf", NT, "act")
        s_kf = items("kf", 24, "act")
        s_vf = items("vf", NT, "dve")
        s_x5T = items("x5T", 8, "act", after=s_xbT)
        s_qk = items("qk", 16, "act")
        s_vb, s_sc, s_pT = stage("vblk", "dve"), stage("scores", "dve"), stage("probT", "act")
        s_pv, s_cx, s_ow = stage("ctx", "dve"), stage("ctxT", "act"), stage("attno", "dve")
        small = 0
        for i in range(NT + 4):
            for s, lag, taker in ((s_vb, 0, "dve"), (s_sc, 0, "dve"), (s_pT, 1, "act"),
                                  (s_pv, 2, "dve"), (s_cx, 3, "act"), (s_ow, 4, "dve")):
                if 0 <= i - lag < NT:
                    if s is s_sc:
                        use(s, [[2, 3], [4, 5]][i % 2], taker)
                    elif s is s_pT:
                        use(s, [6, 7], taker)
                    else:
                        use(s, [small % 2], taker)
                        small += 1
        s_mT = items("mlpT", 8, "act", after=s_x5T)
        s_m1, s_m2 = [items("mlp1", 24, "act")], [items("mlp2", NT, "dve")]
        s_xmT = items("xmT", 8, "act", after=s_mT)
        s_gl = items("gate", 1, "dve")
        for e in range(NX):
            s_m1.append(items("mlp1", 24, "act", after=s_m1[e]))
            s_m2.append(items("mlp2", NT, "dve", after=s_m2[e]))

        loaded = {k: sem(f"loaded_{k}") for k in (
            "tok_w", "p0", "p1", "p2", "p3", "m0", "m1", "alog0", "alog1", "d0", "d1", "wout0", "wout1", "gb", "soft", "w1e0", "w1e1", "w2e0", "w2e1",
            "rw", "rwB", "tb", "mlpw0", "mlpw1")}
        const_ready = sem("const_ready")
        xh_ready = sem("xh_ready")
        conv_done = sem("conv_done")
        xconv_ready = sem("xconv_ready")
        bc_ready = sem("bc_ready")
        abs_done = sem("abs_done")
        r_ready, s_ready, w_ready = sem("r_ready"), sem("s_ready"), sem("w_ready")
        dt_ready, du_ready, dtr_ready = sem("dt_ready"), sem("du_ready"), sem("dtr_ready")
        aneg_exp = sem("aneg_exp")
        aneg_ready = sem("aneg_ready")
        b_filled = sem("b_filled")
        c_filled = sem("c_filled")
        c_ready = sem("c_ready")
        dA_ready = sem("dA_ready")
        times_b = sem("times_b")
        scanned = sem("scanned")
        times_c = sem("times_c")
        summed = sem("summed")
        y_taken = sem("y_taken")
        gated = sem("gated")
        mamba_out = sem("mamba_out")
        dve_steps, act_steps, pool_steps = sem("dve_steps"), sem("act_steps"), sem("pool_steps")
        hb_ready = sem("hb_ready")
        xn_ready = sem("xn_ready")
        phi_ready = sem("phi_ready")
        dexp, dnorm = sem("dexp"), sem("dnorm")
        cexp, cbd_ready = sem("cexp"), sem("cbd_ready")
        ys_stored = [sem(f"ys_stored{k}") for k in range(2)]
        xa_ready, xb_ready = sem("xa_ready"), sem("xb_ready")
        w_args, w_exps = sem("w_args"), sem("w_exps")
        ry_ready = sem("ry_ready")
        kf_ready = sem("kf_ready")
        x5_ready = sem("x5_ready")
        kblk_ready = sem("kblk_ready")
        sexp = sem("sexp")
        comb_sub, comb_exp = sem("comb_sub"), sem("comb_exp")
        xm_ready = sem("xm_ready")
        h_plus = sem("h_plus")
        out_done = sem("out_done")
        block = ctx.enter_context(nc.Block())

        def cols(i):
            return slice(i * TILE, (i + 1) * TILE)

        def quarter(q):
            return slice(q * QT, (q + 1) * QT)

        def gq(buf, c, q):
            return buf[:, (q // 2) * 3 + c, (q % 2) * QT:(q % 2 + 1) * QT]

        def y_bank(g):
            return 6 if g % 3 == 1 else 4

        QH = HID // 2
        EXPS = 7
        KVR = [(w, p, s) for p in range(3) for w in range(3) for s in range(2)]

        def take_xs(eng, i):
            grp, c = divmod(i, 2)
            s_xs.wait_filled(eng, i)
            src = bank(s_xs.banks[i][0], CH, 0, 512).rearrange("p (i n) -> p i n", n=NE)
            dst = xsT[0:CH, c, :, 8 * grp:8 * grp + 8].rearrange("p n i -> p i n")
            eng.tensor_copy(dst, src).then_inc(s_xs.taken["dve"], 1)

        PIECES = ((0, 0, HI), (1, HI, IMAGES), (2, IMAGES, SEG))

        @block.sync
        def _(sp):
            def load(key, dst, src):
                sp.dma_start(dst, src).then_inc(loaded[key], 16)

            load("tok_w", w_tok, a["tok_w"])
            for q in range(NQ):
                load(f"p{q}", patches[:, :, quarter(q)], a["patches"][:, :, quarter(q)])

            def load_mamba(r):
                p = ("fwd", "bwd")[r]
                load(f"m{r}", w_in, a[f"{p}_w_in"])
                load(f"m{r}", taps, a[f"{p}_conv_w"])
                load(f"m{r}", conv_b, a[f"{p}_conv_b"])
                load(f"m{r}", dt_b, a[f"{p}_b_dt"])
                for k in range(3):
                    load(f"m{r}", w_x[:, :, 32 * k:32 * k + 32], a[f"{p}_w_bc"])
                load(f"m{r}", w_x[:, :, 96:108], a[f"{p}_w_dtr"])
                load(f"m{r}", w_dt[96:108, :], a[f"{p}_w_dt"])

            load_mamba(0)
            load("alog0", a_neg, a["fwd_a_log"])
            load("d0", d_skip, a["fwd_d"])
            for r in range(2):
                load(f"wout{r}", w_out[r], a[("fwd", "bwd")[r] + "_w_out"])
            s_dt[0].wait_taken(sp, 11)
            load_mamba(1)
            sp.wait_ge(dA_ready, UNITS)
            load("alog1", a_neg, a["bwd_a_log"])
            sp.wait_ge(gated, GROUPS)
            load("d1", d_skip, a["bwd_d"])
            sp.wait_ge(gated, 2 * GROUPS)
            s_wo[1].wait_filled(sp, NT - 1)
            load("gb", g_row, a["ln_g"].partition_broadcast(TILE))
            load("gb", b_row, a["ln_b"].partition_broadcast(TILE))
            load("soft", phiT, a["phi"])
            load("soft", scale_b, a["scale"].partition_broadcast(NE))
            for g in range(NG + 1):
                if g < NG:
                    b, four = g % 2, slice(EG * g, EG * g + EG)
                    if g >= 2:
                        s_h1.wait_filled(sp, 2 * g - 3)
                    load(f"w1e{b}", w1e[0:CH, b].rearrange("p (e c) n -> p e (c n)", c=2),
                         a["e_w1"][four].rearrange("e (p c) n -> p e (c n)", c=2))
                    load(f"w1e{b}", w1e[CH:CH + 1, b, 1:2 * EG:2], a["e_b1"][four, :].unsqueeze(0))
                if g >= 1:
                    b, four = (g - 1) % 2, slice(EG * (g - 1), EG * g)
                    if g >= 3:
                        s_y2.wait_filled(sp, g - 3)
                    load(f"w2e{b}", w2e[:, b].rearrange("p (e k) n -> p e (k n)", k=HC),
                         a["e_w2"][four].rearrange("e (p k) n -> p e (k n)", k=HC))
                    load(f"w2e{b}", b2e[:, b],
                         a["e_b2"][four, :].rearrange("(o e) n -> o (e n)", o=1))
            s_mix.wait_taken(sp, NT - 1)
            load("rw", w_kvr, a["w_kvr"])
            load("rw", aff[:, 0, :], a["r_ln1_w"])
            load("rw", aff[:, 1, :], a["r_ln1_b"])
            load("rw", aff[:, 2, :], a["r_ln2_w"])
            load("rw", aff[:, 3, :], a["r_ln2_b"])
            for j, name in enumerate(("decay", "first")):
                load("rw", wu[:, 2 * j:2 * j + 1], a[name][0:128, :])
                load("rw", wu[0:64, 2 * j + 1:2 * j + 2], a[name][128:D, :])
                load("rw", wu[64:128, 2 * j + 1:2 * j + 2], a[name][128:D, :])
            load("rwB", w_oA, a["w_o"][0:128, :])
            load("rwB", w_oB[0:64], a["w_o"][128:D, :])
            load("rwB", w_oB[64:128], a["w_o"][128:D, :])
            load("rwB", w_kf, a["w_kf"])
            load("rwB", w_vf, a["w_vf"])
            load("rwB", w_rf, a["w_rf"])
            s_vf.wait_taken(sp, NT - 1)
            sp.wait_ge(h_plus, NT)
            load("tb", in_w[0:CH], a["in_w"])
            load("tb", in_w[CH:CH + 1, 1, :], a["in_b"])
            load("tb", o_w[0:CH], a["out_w"])
            load("tb", o_w[CH:CH + 1, 1, :], a["out_b"])
            load("tb", gate_w[0:CH], a["gate_w"])
            load("tb", gate_w[CH:CH + 1, 1, :], a["gate_b"])
            load("tb", aff5[:, 0, :], a["t_ln1_g"])
            load("tb", aff5[:, 1, :], a["t_ln1_b"])
            load("tb", aff5[:, 2, :], a["t_ln2_g"])
            load("tb", aff5[:, 3, :], a["t_ln2_b"])
            for e in range(NX + 1):
                if e >= 2:
                    s_m1[e - 2].wait_filled(sp, 23)
                    s_m2[e - 2].wait_taken(sp, NT - 1)
                b, key = e % 2, f"mlpw{e % 2}"
                load(key, mlp1[b][0:CH], a[f"mlp_w1_{e}"])
                load(key, mlp1[b][CH:CH + 1, 1, :], a[f"mlp_b1_{e}"])
                load(key, mlp2[b], a[f"mlp_w2_{e}"])
                load(key, mlp2b[b], a[f"mlp_b2_{e}"].partition_broadcast(TILE))
            for i in range(NT):
                s_m2[NX].wait_taken(sp, i)
                sp.dma_start(out[:, i, :], h[:, i, :]).then_inc(out_done, 16)
            sp.wait_ge(out_done, 16 * NT)

        @block.gpsimd
        def _(pool):
            own = Steps(pool, pool_steps)
            own.then(pool.memset(ident[:, :], 0.0))
            pool.affine_select(out=ident[:, :], in_=ident[:, :], compare_op=ALU.not_equal, fill=1.0,
                               base=0, pattern=[[-1, 128]], channel_multiplier=1).then_inc(const_ready, 1)
            own.step(pool.memset(two_p[:, :], 2.0))
            pool.memset(ones[:, :], 1.0).then_inc(const_ready, 1)
            own.then(pool.memset(sel, 0.0))
            for k in range(3):
                ins = pool.affine_select(out=sel, in_=sel, compare_op=ALU.not_equal, fill=1.0,
                                         base=-32 * k, pattern=[[-1, 2 * NS], [0, 128]],
                                         channel_multiplier=1)
                if k < 2:
                    own.then(ins)
            ins.then_inc(const_ready, 1)

            def du_of(r, c):
                pool.wait_ge(dt_ready, r * 3 + c + 1)
                pool.tensor_tensor(du[:, c:GROUPS:3, :], dt[:, c:GROUPS:3, :], xconv[:, c:GROUPS:3, :],
                                   ALU.mult).then_inc(du_ready, 1)

            for r in range(2):
                edge = 0 if r == 0 else TOKENS - 1
                if r == 1:
                    pool.wait_ge(scanned, UNITS)
                for c in range(4):
                    if c == 3 or c == 2:
                        du_of(r, c - 2)
                    if c < 3:
                        pool.wait_ge(r_ready, r * 3 + c + 1)
                        pool.tensor_tensor(soft_e[:, c % 2, :], soft_e[:, c % 2, :], soft_r[:, c % 2, :],
                                           ALU.mult).then_inc(s_ready, 1)
                du_of(r, 2)
                for k in range(2):
                    pool.memset(dA[:, k, :].rearrange("p (i l) -> p i l", l=TOKENS)[:, :, edge:edge + 1],
                                0.0).then_inc(const_ready, 1)
                for n in range(UNITS):
                    u = r * UNITS + n
                    if n // NS % 3 == 0:
                        pool.wait_ge(c_ready, (r * 2 + n // NS // 3) * NS + n % NS + 1)
                    pool.wait_ge(scanned, u + 1)
                    pool.tensor_tensor(hbuf[:, u % SLOTS, :], hbuf[:, u % SLOTS, :], c_all[:, n % NS, :],
                                       ALU.mult).then_inc(times_c, 1)
            pool.wait_ge(loaded["gb"], 32)
            for i in range(NT):
                pool.tensor_tensor(hb[:, i, :], h[:, i, :], b_row, ALU.add).then_inc(hb_ready, 1)
            pool.wait_ge(mamba_out, NT)
            own.then(pool.memset(mask2, 1.0))
            own.then(pool.affine_select(out=mask2[:, 0, :], in_=mask2[:, 0, :], compare_op=ALU.is_ge,
                                        fill=0.0, base=TOKENS - 1, pattern=[[0, NE]],
                                        channel_multiplier=-1))
            pool.affine_select(out=mask2[:, 1, :], in_=mask2[:, 1, :], compare_op=ALU.is_ge, fill=0.0,
                               base=-TOKENS, pattern=[[0, NE]], channel_multiplier=1)\
                .then_inc(const_ready, 1)
            pool.wait_ge(const_ready, MIX_CONST - 1)
            pool.memset(xsT[CH:CH + 1, 1, :, :], 1.0).then_inc(const_ready, 1)
            s_mix.wait_taken(pool, NT - 1)
            for r in range(2):
                edge = 0 if r == 0 else TOKENS - 1
                own.then(pool.memset(step_w[r], 0.0))
                own.then(pool.memset(step_w[r].rearrange("p (s l) -> p s l", l=TOKENS)[:, :, edge:edge + 1],
                                     -1e38))
                for s in (m_s, a_s, b_s):
                    cells = s[r][:, 0:1] if r == 0 else s[r][:, HALF:W + 1:HALF]
                    ins = pool.memset(cells, 0.0)
                    if r == 1 and s is b_s:
                        ins.then_inc(const_ready, 1)
                    else:
                        own.then(ins)
            for i in range(NT):
                s_vf.wait_taken(pool, i)
                pool.tensor_tensor(h[:, i, :], h[:, i, :], x1[:, i, :], ALU.add).then_inc(h_plus, 1)
            pool.wait_ge(h_plus, NT)
            own.then(pool.memset(x5T[CH:CH + 1, 1, :], 1.0))
            own.then(pool.memset(x5two[CH:CH + 1, 1, :], 1.0))
            own.then(pool.memset(ctxT[CH:CH + 1, 1, :], 1.0))
            own.then(pool.memset(kmask, 1.0))
            own.then(pool.affine_select(out=kmask, in_=kmask, compare_op=ALU.is_ge, fill=0.0, base=0,
                                        pattern=[[-HD, 6]], channel_multiplier=1))
            own.then(pool.affine_select(out=kmask, in_=kmask, compare_op=ALU.is_ge, fill=0.0,
                                        base=HD - 1, pattern=[[HD, 6]], channel_multiplier=-1))
            vm = vmask.rearrange("p (g o) d -> p g o d", o=2)
            own.then(pool.memset(vmask, 1.0))
            for g in range(6):
                own.then(pool.affine_select(out=vm[:, g, 0, :], in_=vm[:, g, 0, :], compare_op=ALU.is_ge,
                                            fill=0.0, base=TOKENS - 1, pattern=[[0, HD]],
                                            channel_multiplier=-1))
                ins = pool.affine_select(out=vm[:, g, 1, :], in_=vm[:, g, 1, :], compare_op=ALU.is_ge,
                                         fill=0.0, base=-TOKENS, pattern=[[0, HD]],
                                         channel_multiplier=1)
                if g < 5:
                    own.then(ins)
            ins.then_inc(const_ready, 1)
            for i in range(NT):
                last = min(2 * i * TOKENS + TILE - 1, T - 1) // QT
                s_qk.wait_taken(pool, 4 * last + 3)
                if i >= 2:
                    s_sc.wait_filled(pool, i - 2)
                for j in range(2):
                    for c in range(2):
                        at = (2 * i + j) * TOKENS
                        pool.tensor_tensor(
                            kblk[:, 4 * (i % 2) + 2 * j + c, :].rearrange("p (h l) -> p h l", l=TOKENS),
                            kT[:, c, at:at + TOKENS].unsqueeze(1).broadcast_to([CH, 6, TOKENS]),
                            kmask.unsqueeze(2).broadcast_to([CH, 6, TOKENS]), ALU.mult)\
                            .then_inc(kblk_ready, 1)
            for i in range(NT):
                s_m2[0].wait_taken(pool, i)
                pool.tensor_tensor(h[:, i, :], h[:, i, :], x5[:, i, :], ALU.add).then_inc(h_plus, 1)

        @block.scalar
        def _(act):
            own = Steps(act, act_steps)

            def copy_out(s, i, dst, src, func=ACT.Copy, **kw):
                s.wait_filled(act, i)
                act.activation(dst, src, func, **kw).then_inc(s.taken["act"], 1)

            for i in range(NT):
                copy_out(s_tok, i, h[:, i, :], bank(s_tok.banks[i][0], TILE, 0, D))
            for i in range(8):
                q, c = divmod(i, 2)
                copy_out(s_xhT, i, xhT[:, c, quarter(q)], bank(s_xhT.banks[i][0], CH, 0, QT))
            for r in range(2):
                act.wait_ge(loaded[f"alog{r}"], 16)
                act.activation(a_neg, a_neg, ACT.Exp).then_inc(aneg_exp, 1)
                if r == 1:
                    act.wait_ge(times_c, UNITS)
                    s_wo[0].wait_filled(act, NT - 1)
                    act.wait_ge(gated, GROUPS)
                at = TAPS - 1 if r == 0 else 0
                for i in range(24):
                    q, m = divmod(i, 6)
                    src = bank(s_xz[r].banks[i][0], 128, 0, QT)
                    if m < 3:
                        copy_out(s_xz[r], i, xc[:, m, 8 * q:8 * q + 8, at:at + TOKENS],
                                 src.rearrange("p (i l) -> p i l", l=TOKENS))
                    else:
                        copy_out(s_xz[r], i, gq(zs, m - 3, q), src, ACT.Silu)
                for q in range(NQ):
                    for c in range(3):
                        act.wait_ge(conv_done, r * 12 + q * 3 + c + 1)
                        act.activation(gq(xconv, c, q), gq(du, c, q), ACT.Silu).then_inc(xconv_ready, 1)
                act.wait_ge(const_ready, 2)
                for c in range(4):
                    if c < 3:
                        e_c, r_c = soft_e[:, c % 2, :], soft_r[:, c % 2, :]
                        if c == 2:
                            act.wait_ge(dt_ready, r * 3 + 1)
                        act.wait_ge(abs_done, r * 3 + c + 1)
                        own.then(act.activation(e_c, e_c, ACT.Exp))
                        own.then(act.activation(r_c, e_c, ACT.Ln, bias=two_p[:, 0:1]))
                        act.activation(r_c, r_c, ACT.Exp, scale=-1.0).then_inc(r_ready, 1)
                    if c >= 1:
                        k = c - 1
                        e_c, r_c = soft_e[:, k % 2, :], soft_r[:, k % 2, :]
                        act.wait_ge(s_ready, r * 3 + k + 1)
                        own.then(act.activation(r_c, e_c, ACT.Square))
                        act.activation(soft_w[:, k % 2, :], r_c, ACT.Copy, scale=ATANH[4])\
                            .then_inc(w_ready, 1)
                act.wait_ge(aneg_ready, r + 1)
                act.wait_ge(du_ready, 3 * r + 3)
                act.wait_ge(const_ready, 5 + 2 * r)
                lo = 1 if r == 0 else 0
                for n in range(UNITS):
                    u, g, j = r * UNITS + n, n // NS, n % NS
                    if u >= 2:
                        act.wait_ge(scanned, u - 1)
                    act.activation(
                        dA[:, u % 2, :].rearrange("p (i l) -> p i l", l=TOKENS)[:, :, lo:lo + TOKENS - 1],
                        dt[:, g, :].rearrange("p (i l) -> p i l", l=TOKENS)[:, :, lo:lo + TOKENS - 1],
                        ACT.Exp, scale=a_neg[:, (g % 3) * NS + j:(g % 3) * NS + j + 1])\
                        .then_inc(dA_ready, 1)
                    if g % 3 == 0:
                        act.wait_ge(c_filled, (r * 2 + g // 3) * NS + j + 1)
                        if g == 3:
                            act.wait_ge(times_c, r * UNITS + 2 * NS + j + 1)
                        act.activation(c_all[:, j, :], two(6, 128, HALF), ACT.Copy).then_inc(c_ready, 1)
            for c in range(2):
                copy_out(s_phi, c, phin[:, c, :], bank(s_phi.banks[c][0], CH, 0, NE))
            for i in range(8):
                q, c = divmod(i, 2)
                copy_out(s_xnT, i, xnT[:, c, quarter(q)], bank(s_xnT.banks[i][0], CH, 0, QT))
            for q in range(NQ):
                s_dl.wait_taken(act, q)
                v = dlog[:, 8 * q:8 * q + 8, :]
                act.activation(v, v, ACT.Exp).then_inc(dexp, 1)
            for k in range(2):
                s_cl.wait_taken(act, k)
                v = clog[:, 8 * k:8 * k + 8, :]
                act.activation(v, v, ACT.Exp).then_inc(cexp, 1)
            for i in range(NT):
                copy_out(s_cT, i, cT[:, i, :], bank(s_cT.banks[i][0], 128, 0, TILE))

            def expert_out(g):
                if g >= 2:
                    act.wait_ge(ys_stored[g % 2], 16 * 8 * (g // 2))
                copy_out(s_y2, g, ys[:, g % 2, :], bank(s_y2.banks[g][0], 128, 0, D))
                s_y2.wait_taken(act, g)
                for j in range(EG):
                    for par in range(2):
                        e = par * NE + EG * g + j
                        act.dma_start(ysN[e:e + 1, :, :], ys[32 * j + par:32 * j + 32:2, g % 2, :])\
                            .then_inc(ys_stored[g % 2], 16)

            for g in range(NG + 1):
                if g < NG:
                    for k in range(2):
                        if g >= 2 and k == 0:
                            s_hT.wait_filled(act, 2 * (g - 2) + 1)
                        i = 2 * g + k
                        copy_out(s_h1, i, hid_e[:, g % 2, k * QH:(k + 1) * QH],
                                 bank(s_h1.banks[i][0], 128, 0, QH), ACT.Gelu)
                if g >= 2:
                    expert_out(g - 2)
            expert_out(NG - 1)
            act.wait_ge(loaded["rw"], 16 * 11)
            for i in range(8):
                q, c = divmod(i, 2)
                copy_out(s_xaT, i, xaT[:, c, quarter(q)], bank(s_xaT.banks[i][0], CH, 0, QT),
                         ACT.Identity, bias=aff[:, 1, c:c + 1], scale=aff[:, 0, c:c + 1])
            for i in range(18):
                which, piece, part = KVR[i]
                dst = (kk, vv, sr)[which][:, piece * HALF + part * QT:piece * HALF + (part + 1) * QT]
                copy_out(s_kvr, i, dst, bank(s_kvr.banks[i][0], 128, 0, QT),
                         ACT.Sigmoid if which == 2 else ACT.Copy)
            for p in range(3):
                for n in range(EXPS):
                    act.wait_ge(w_args, EXPS * p + n + 1)
                    act.activation(ex[:, n, :], ex[:, n, :], ACT.Exp).then_inc(w_exps, 1)
            for i in range(8):
                q, c = divmod(i, 2)
                copy_out(s_xbT, i, xaT[:, c, quarter(q)], bank(s_xbT.banks[i][0], CH, 0, QT),
                         ACT.Identity, bias=aff[:, 3, c:c + 1], scale=aff[:, 2, c:c + 1])
            for i in range(NT):
                copy_out(s_rf, i, sig[:, i, :], bank(s_rf.banks[i][0], TILE, 0, D), ACT.Sigmoid)
            for i in range(24):
                if i >= 4:
                    act.wait_ge(kf_ready, i - 3)
                copy_out(s_kf, i, relu_b[:, i % 4, :], bank(s_kf.banks[i][0], 128, 0, QT), ACT.Relu)
            act.wait_ge(loaded["tb"], 16 * 10)
            for i in range(8):
                q, c = divmod(i, 2)
                src = bank(s_x5T.banks[i][0], CH, 0, QT)
                s_x5T.wait_filled(act, i)
                act.activation(x5two[0:CH, c, 2 * q * QT:2 * (q + 1) * QT]
                               .rearrange("p (i o l) -> p i o l", o=2, l=TOKENS),
                               src.rearrange("p (i l) -> p i l", l=TOKENS).unsqueeze(2)
                               .broadcast_to([CH, 8, 2, TOKENS]),
                               ACT.Identity, bias=aff5[:, 1, c:c + 1], scale=aff5[:, 0, c:c + 1])
                copy_out(s_x5T, i, x5T[0:CH, c, quarter(q)], src,
                         ACT.Identity, bias=aff5[:, 1, c:c + 1], scale=aff5[:, 0, c:c + 1])
            for i in range(16):
                q, which, c = i // 4, i // 2 % 2, i % 2
                dst = (qT[:, c, quarter(q)], kT[:, c, quarter(q)])[which]
                copy_out(s_qk, i, dst, bank(s_qk.banks[i][0], CH, 0, QT))

            def probs(i):
                s_sc.wait_taken(act, i)
                act.activation(prob[:, i % 2], prob[:, i % 2], ACT.Exp, scale=HD ** -0.5)\
                    .then_inc(sexp, 1)

            def probs_t(i):
                if i >= 4:
                    s_pv.wait_filled(act, i - 4)
                copy_out(s_pT, i, probT[:, 6 * (i % 4):6 * (i % 4) + 6, :].rearrange("p (b g) q -> p b g q", b=2),
                         psum[3][0:TILE, :].rearrange("p (b n) -> p b n", b=2)[:, :, 0:3 * PAIR]
                         .rearrange("p b (g q) -> p b g q", q=PAIR))

            def ctx_t(i):
                v = bank(s_cx.banks[i][0], CH, 0, 2 * 128).rearrange("p (c j q) -> p c j q", c=2, j=2)
                copy_out(s_cx, i, ctxT[0:CH, :, cols(i)].rearrange("p c (j l) -> p c j l", j=2),
                         v[:, :, :, 0:TOKENS])

            for i in range(NT + 3):
                if i < NT:
                    probs(i)
                if 1 <= i <= NT:
                    probs_t(i - 1)
                if i >= 3:
                    ctx_t(i - 3)
            for i in range(8):
                q, c = divmod(i, 2)
                copy_out(s_mT, i, x5T[0:CH, c, quarter(q)], bank(s_mT.banks[i][0], CH, 0, QT))

            def hidden(e):
                s = s_m1[e]
                for i in range(24):
                    q, m = divmod(i, 6)
                    if e >= 2 and m == 0:
                        s_m2[e - 2].wait_filled(act, 4 * q + 3)
                    copy_out(s, i, hid[e % 2][:, m, quarter(q)], bank(s.banks[i][0], 128, 0, QT),
                             ACT.Gelu)

            hidden(0)
            for i in range(8):
                q, c = divmod(i, 2)
                copy_out(s_xmT, i, x5T[0:CH, c, quarter(q)], bank(s_xmT.banks[i][0], CH, 0, QT),
                         ACT.Identity, bias=aff5[:, 3, c:c + 1], scale=aff5[:, 2, c:c + 1])
            act.wait_ge(comb_sub, 1)
            act.activation(comb, comb, ACT.Exp).then_inc(comb_exp, 1)
            for e in range(1, NX + 1):
                hidden(e)


        @block.vector
        def _(dve):
            own = Steps(dve, dve_steps)
            TS, TT, STT = dve.tensor_scalar, dve.tensor_tensor, dve.scalar_tensor_tensor

            def rsqrt(dst, x, tmp):
                own.then(TS(dst.bitcast(I32), x.bitcast(I32), 1, None, ALU.logical_shift_right))
                own.then(TS(dst.bitcast(I32), dst.bitcast(I32), -1.0, RSQRT_MAGIC, ALU.mult, ALU.add))
                for _ in range(3):
                    own.then(STT(tmp, x, -0.5, dst, ALU.mult, ALU.mult))
                    own.then(TT(tmp, tmp, dst, ALU.mult))
                    own.then(STT(dst, tmp, 1.5, dst, ALU.add, ALU.mult))

            def norm_stats(src, k, ready):
                ks = slice(8 * k, 8 * k + 8)
                own.wait()
                for t in range(8):
                    ready(8 * k + t)
                    own.step(dve.bn_stats(stats[:, t, :], src[:, 8 * k + t, :]))
                own.wait()
                for t in range(8):
                    own.step(dve.bn_aggr(mv[:, 8 * k + t, :], stats[:, t, :]))
                own.wait()
                own.then(TS(lnv[:, ks], mv[:, ks, 1], LN_EPS, None, ALU.add))
                rsqrt(rstd[:, ks], lnv[:, ks], lnw[:, ks])

            def normalise(dst, src, i, factor):
                return TS(dst[:, i, :], src[:, i, :], mv[:, i, 0:1], factor[:, i:i + 1],
                          ALU.subtract, ALU.mult)

            def twice_normed(src, once, again, ready, signal):
                for k in range(2):
                    ks = slice(8 * k, 8 * k + 8)
                    norm_stats(src, k, ready)
                    own.then(TT(sc1[:, ks], mv[:, ks, 1], rstd[:, ks], ALU.mult))
                    own.then(TT(sc1[:, ks], sc1[:, ks], rstd[:, ks], ALU.mult))
                    own.then(TS(sc1[:, ks], sc1[:, ks], LN_EPS, None, ALU.add))
                    rsqrt(sc2[:, ks], sc1[:, ks], lnw[:, ks])
                    own.then(TT(sc2[:, ks], sc2[:, ks], rstd[:, ks], ALU.mult))
                    for i in range(8 * k, 8 * k + 8):
                        own.step(normalise(once, src, i, rstd))
                        normalise(again, src, i, sc2).then_inc(signal, 1)

            for k in range(2):
                norm_stats(h, k, lambda i: s_tok.wait_taken(dve, i))
                for i in range(8 * k, 8 * k + 8):
                    normalise(xh, h, i, rstd).then_inc(xh_ready, 1)

            for r in range(2):
                dve.wait_ge(aneg_exp, r + 1)
                TS(a_neg, a_neg, -1.0, None, ALU.mult).then_inc(aneg_ready, 1)
                if r == 1:
                    dve.wait_ge(times_c, UNITS)
                pad = (0, TAPS - 1) if r == 0 else (TOKENS, PAD)
                for c in range(3):
                    own.step(dve.memset(xc[:, c, :, pad[0]:pad[1]], 0.0))
                own.wait()
                dve.wait_ge(loaded[f"m{r}"], 16 * 9)
                for q in range(NQ):
                    s_xz[r].wait_taken(dve, 6 * q + 2)
                    for k in range(TAPS):
                        at = k if r == 0 else TAPS - 1 - k
                        for c in range(3):
                            x_k = xc[:, c, 8 * q:8 * q + 8, at:at + TOKENS]
                            acc = gq(du, c, q).rearrange("p (i l) -> p i l", l=TOKENS)
                            if k == 0:
                                own.step(TS(acc, x_k, taps[:, c, 0:1], conv_b[:, c:c + 1],
                                            ALU.mult, ALU.add))
                            else:
                                ins = STT(acc, x_k, taps[:, c, k:k + 1], acc, ALU.mult, ALU.add)
                                if k < TAPS - 1:
                                    own.step(ins)
                                else:
                                    ins.then_inc(conv_done, 1)
                        own.wait()
                for q in range(NQ):
                    s_xp[r].wait_filled(dve, q)
                    dve.tensor_copy(dtr[96:108, quarter(q)], bank(s_xp[r].banks[q][0], 108, 0, QT, 96))\
                        .then_inc(dtr_ready, 1)

                def split_bc():
                    for q in range(NQ):
                        ps = bank(s_xp[r].banks[q][0], 108, 0, QT)
                        qs = quarter(q)
                        own.then(dve.tensor_copy(bc[:, qs], ps[0:96]))
                        TT(res[0:64, q % 2, :], ps[0:64], bc[0:64, qs], ALU.subtract)\
                            .then_inc(s_xp[r].taken["dve"], 1)
                        s_xp[r].wait_taken(dve, q)
                        own.then(dve.tensor_copy(bc[0:64, qs], res[0:64, q % 2, :]))
                        TT(bc[0:32, qs], res[0:32, q % 2, :], bc[0:32, qs], ALU.subtract)\
                            .then_inc(bc_ready, 1)

                def step_size(c):
                    if c == 2:
                        dve.wait_ge(dt_ready, 3 * r + 1)
                    for q in range(NQ):
                        i = 4 * c + q
                        s_dt[r].wait_filled(dve, i)
                        TS(soft_y[:, c % 2, quarter(q)], bank(s_dt[r].banks[i][0], 128, 0, QT),
                           dt_b[:, c:c + 1], None, ALU.add).then_inc(s_dt[r].taken["dve"], 1)
                    s_dt[r].wait_taken(dve, 4 * c + 3)
                    STT(soft_e[:, c % 2, :], soft_y[:, c % 2, :], -1.0, soft_y[:, c % 2, :],
                        ALU.mult, ALU.min).then_inc(abs_done, 1)

                def inputs_of_scan(c):
                    s_c, sq_c, w_c = soft_e[:, c % 2, :], soft_r[:, c % 2, :], soft_w[:, c % 2, :]
                    dve.wait_ge(w_ready, r * 3 + c + 1)
                    for k in (3, 2, 1):
                        own.then(STT(w_c, w_c, ATANH[k], sq_c, ALU.add, ALU.mult))
                    own.then(STT(w_c, w_c, ATANH[0], s_c, ALU.add, ALU.mult))
                    y2, l2 = (v[:, c % 2, :].rearrange("p (h t) -> p h t", h=2) for v in (soft_y, soft_w))
                    STT(dt[:, c:GROUPS:3, :], y2, 0.0, l2, ALU.max, ALU.add).then_inc(dt_ready, 1)

                step_size(0)
                step_size(1)
                split_bc()
                inputs_of_scan(0)
                step_size(2)
                inputs_of_scan(1)
                inputs_of_scan(2)

                def times_B(n):
                    u = r * UNITS + n
                    dve.wait_ge(b_filled, u + 1)
                    if u >= SLOTS:
                        dve.wait_ge(summed, u - SLOTS + 1)
                    TT(hbuf[:, u % SLOTS, :], two(2 * (u % 2), 128, HALF), du[:, n // NS, :],
                       ALU.mult).then_inc(times_b, 1)

                def scan(n):
                    u = r * UNITS + n
                    way = slice(None, None, 1 if r == 0 else -1)
                    dve.wait_ge(times_b, u + 1)
                    dve.wait_ge(dA_ready, u + 1)
                    dve.tensor_tensor_scan(hbuf[:, u % SLOTS, :][:, way], dA[:, u % 2, :][:, way],
                                           hbuf[:, u % SLOTS, :][:, way], 0.0,
                                           ALU.mult, ALU.add).then_inc(scanned, 1)

                def gate_output(g):
                    dve.wait_ge(loaded[f"d{r}"], 16)
                    dve.wait_ge(summed, r * UNITS + NS * (g + 1))
                    STT(xconv[:, g, :], xconv[:, g, :], d_skip[:, g % 3:g % 3 + 1], two(y_bank(g), 128, HALF),
                        ALU.mult, ALU.add).then_inc(y_taken, 1)
                    dve.wait_ge(y_taken, r * GROUPS + g + 1)
                    TT(zs[:, g, :], zs[:, g, :], xconv[:, g, :], ALU.mult).then_inc(gated, 1)

                dve.wait_ge(du_ready, 3 * r + 3)
                times_B(0)
                for n in range(UNITS):
                    if n + 1 < UNITS:
                        times_B(n + 1)
                    scan(n)
                    g = n // NS - 1
                    if g >= 0 and n % NS == (2 if y_bank(g) == y_bank(g + 1) else 6):
                        gate_output(g)
                gate_output(GROUPS - 1)
                for i in range(NT):
                    if r == 1:
                        s_wo[0].wait_taken(dve, i)
                    s_wo[r].wait_filled(dve, i)
                    TT(xh[:, i, :], xh[:, i, :], bank(s_wo[r].banks[i][0], TILE, 0, D), ALU.add)\
                        .then_inc(s_wo[r].taken["dve"], 1)

            for k in range(2):
                norm_stats(xh, k, lambda i: s_wo[1].wait_taken(dve, i))
                dve.wait_ge(loaded["gb"], 32)
                for i in range(8 * k, 8 * k + 8):
                    own.step(STT(zln[:, i, :], xh[:, i, :], mv[:, i, 0:1], g_row, ALU.subtract, ALU.mult))
                own.wait()
                for i in range(8 * k, 8 * k + 8):
                    dve.wait_ge(hb_ready, i + 1)
                    STT(h[:, i, :], zln[:, i, :], rstd[:, i:i + 1], hb[:, i, :], ALU.mult, ALU.add)\
                        .then_inc(mamba_out, 1)

            dve.wait_ge(loaded["soft"], 32)
            own.then(TT(phi_sq, phiT, phiT, ALU.mult))
            own.then(dve.tensor_reduce(phi_n[:, 0:1], phi_sq, AX.X, ALU.add))
            rsqrt(phi_n[:, 1:2], phi_n[:, 0:1], phi_n[:, 2:3])
            own.then(TT(phi_n[:, 3:4], phi_n[:, 0:1], phi_n[:, 1:2], ALU.mult))
            own.then(TS(phi_n[:, 3:4], phi_n[:, 3:4], 1e-12, None, ALU.max))
            own.then(dve.reciprocal(phi_n[:, 4:5], phi_n[:, 3:4]))
            TS(phiT, phiT, phi_n[:, 4:5], scale_b[:, 0:1], ALU.mult, ALU.mult).then_inc(phi_ready, 1)
            for k in range(2):
                ks = slice(8 * k, 8 * k + 8)
                norm_stats(h, k, lambda i: dve.wait_ge(mamba_out, i + 1))
                own.then(TS(sc1[:, ks], mv[:, ks, 1], float(D), None, ALU.mult))
                rsqrt(sc2[:, ks], sc1[:, ks], lnw[:, ks])
                own.then(TT(sc2[:, ks], sc2[:, ks], sc1[:, ks], ALU.mult))
                own.then(TT(sc2[:, ks], sc2[:, ks], rstd[:, ks], ALU.mult))
                own.then(TS(sc2[:, ks], sc2[:, ks], 1e-12, None, ALU.max))
                own.then(dve.reciprocal(sc1[:, ks], sc2[:, ks]))
                own.then(TT(sc1[:, ks], sc1[:, ks], rstd[:, ks], ALU.mult))
                for i in range(8 * k, 8 * k + 8):
                    normalise(xn, h, i, sc1).then_inc(xn_ready, 1)
            for q in range(NQ):
                s_dl.wait_filled(dve, q)
                im = slice(8 * q, 8 * q + 8)
                ps = bank(s_dl.banks[q][0], NE, 0, QT).rearrange("p (i l) -> p i l", l=TOKENS)
                own.then(dve.tensor_reduce(dmax[:, im], ps, AX.X, ALU.max))
                TT(dlog[:, im, :], ps, dmax[:, im].unsqueeze(2).broadcast_to([NE, 8, TOKENS]),
                   ALU.subtract).then_inc(s_dl.taken["dve"], 1)
            for k in range(2):
                s_cl.wait_filled(dve, k)
                ts = slice(8 * k, 8 * k + 8)
                ps = bank(s_cl.banks[k][0], TILE, 0, 8 * NE).rearrange("p (t n) -> p t n", n=NE)
                own.then(dve.tensor_reduce(cmax[:, ts], ps, AX.X, ALU.max))
                TT(clog[:, ts, :], ps, cmax[:, ts].unsqueeze(2).broadcast_to([TILE, 8, NE]),
                   ALU.subtract).then_inc(s_cl.taken["dve"], 1)
            for q in range(NQ):
                im = slice(8 * q, 8 * q + 8)
                dve.wait_ge(dexp, q + 1)
                own.then(dve.tensor_reduce(dsum[:, im], dlog[:, im, :], AX.X, ALU.add))
                own.then(dve.reciprocal(dmax[:, im], dsum[:, im]))
                TT(dlog[:, im, :], dlog[:, im, :], dmax[:, im].unsqueeze(2).broadcast_to([NE, 8, TOKENS]),
                   ALU.mult).then_inc(dnorm, 1)
            dve.wait_ge(const_ready, MIX_CONST)
            for i in range(NT):
                s_dT.wait_filled(dve, i)
                ps = bank(s_dT.banks[i][0], TILE, 0, NE)
                TT(dbd[:, i, :].rearrange("p (j n) -> p j n", j=2),
                   ps.unsqueeze(1).broadcast_to([TILE, 2, NE]), mask2, ALU.mult)\
                    .then_inc(s_dT.taken["dve"], 1)
            for k in range(2):
                ts = slice(8 * k, 8 * k + 8)
                dve.wait_ge(cexp, k + 1)
                own.then(dve.tensor_reduce(csum[:, ts], clog[:, ts, :], AX.X, ALU.add))
                own.then(dve.reciprocal(cmax[:, ts], csum[:, ts]))
                own.then(TT(clog[:, ts, :], clog[:, ts, :],
                            cmax[:, ts].unsqueeze(2).broadcast_to([TILE, 8, NE]), ALU.mult))
            for i in range(NT):
                if i >= 2:
                    s_cT.wait_filled(dve, i - 2)
                TT(cbd[:, i % 2, :].rearrange("p (j n) -> p j n", j=2),
                   clog[:, i, :].unsqueeze(1).broadcast_to([TILE, 2, NE]), mask2, ALU.mult)\
                    .then_inc(cbd_ready, 1)
            for i in range(8):
                take_xs(dve, i)
            for g in range(NG):
                for k in range(2):
                    i = 2 * g + k
                    s_hT.wait_filled(dve, i)
                    if g >= 2:
                        s_y2.wait_filled(dve, g - 2)
                    dve.tensor_copy(hidT[:, g % 2, 3 * k:3 * k + 3, :].rearrange("p k n -> p (k n)"),
                                    bank(s_hT.banks[i][0], 128, 0, 384)).then_inc(s_hT.taken["dve"], 1)
            for i in range(NT):
                s_mix.wait_filled(dve, i)
                TT(h[:, i, :], h[:, i, :], bank(s_mix.banks[i][0], TILE, 0, D), ALU.add)\
                    .then_inc(s_mix.taken["dve"], 1)

            twice_normed(h, x1, xa, lambda i: s_mix.wait_taken(dve, i), xa_ready)
            dve.wait_ge(loaded["rw"], 16 * RW_LOADS)
            own.then(TS(wu49, wu, 1.0 / TOKENS, None, ALU.mult))
            dve.wait_ge(const_ready, MIX_CONST + 1)
            for r in range(2):
                own.step(TS(step_w[r][:, 0:T], step_w[r][:, 0:T], wu49[:, 0:1], None, ALU.add))
                own.step(TS(step_w[r][:, T:W], step_w[r][:, T:W], wu49[:, 1:2], None, ALU.add))
            own.wait()
            for p in range(3):
                lo, hi = p * HALF, (p + 1) * HALF
                k_p, v_p = kk[:, lo:hi], vv[:, lo:hi]
                u_p = wu49[:, 2 + p // 2:3 + p // 2]
                now = [[s[r][:, lo + 1 - r:hi + 1 - r] for r in range(2)] for s in (m_s, a_s, b_s)]
                before = [[s[r][:, lo + r:hi + r] for r in range(2)] for s in (m_s, a_s, b_s)]

                def way(v, r):
                    return v[:, ::1 if r == 0 else -1]

                s_kvr.wait_taken(dve, 6 * p + 1)
                for r in range(2):
                    own.step(dve.tensor_tensor_scan(way(now[0][r], r), way(step_w[r][:, lo:hi], r),
                                                    way(k_p, r), 0.0, ALU.add, ALU.max))
                own.wait()
                for r in range(2):
                    own.step(TT(ex[:, 2 * r, :], before[0][r], now[0][r], ALU.subtract))
                own.wait()
                for r in range(2):
                    TT(ex[:, 2 * r, :], ex[:, 2 * r, :], step_w[r][:, lo:hi], ALU.add).then_inc(w_args, 1)
                    TT(ex[:, 2 * r + 1, :], k_p, now[0][r], ALU.subtract).then_inc(w_args, 1)
                dve.wait_ge(w_args, EXPS * p + 4)
                for r in range(2):
                    edge = 0 if r == 0 else TOKENS - 1
                    own.step(dve.memset(before[0][r].rearrange("p (s l) -> p s l", l=TOKENS)
                                        [:, :, edge:edge + 1], -1e38))
                own.wait()
                own.then(TT(ex[:, 8, :], before[0][0], before[0][1], ALU.max))
                own.then(STT(ex[:, 8, :], k_p, u_p, ex[:, 8, :], ALU.add, ALU.max))
                TT(ex[:, 4, :], before[0][0], ex[:, 8, :], ALU.subtract).then_inc(w_args, 1)
                TT(ex[:, 5, :], before[0][1], ex[:, 8, :], ALU.subtract).then_inc(w_args, 1)
                STT(ex[:, 6, :], k_p, u_p, ex[:, 8, :], ALU.add, ALU.subtract).then_inc(w_args, 1)
                s_kvr.wait_taken(dve, 6 * p + 3)
                for r in range(2):
                    dve.wait_ge(w_exps, EXPS * p + 2 * r + 2)
                    own.step(dve.tensor_tensor_scan(way(now[2][r], r), way(ex[:, 2 * r, :], r),
                                                    way(ex[:, 2 * r + 1, :], r), 0.0, ALU.mult, ALU.add))
                    own.then(TT(ex[:, 7, :], ex[:, 2 * r + 1, :], v_p, ALU.mult))
                    own.then(dve.tensor_tensor_scan(way(now[1][r], r), way(ex[:, 2 * r, :], r),
                                                    way(ex[:, 7, :], r), 0.0, ALU.mult, ALU.add))
                dve.wait_ge(w_exps, EXPS * p + 7)
                own.step(TT(ex[:, 0, :], ex[:, 4, :], before[1][0], ALU.mult))
                own.step(TT(ex[:, 1, :], ex[:, 5, :], before[1][1], ALU.mult))
                own.step(TT(ex[:, 2, :], ex[:, 4, :], before[2][0], ALU.mult))
                own.step(TT(ex[:, 3, :], ex[:, 5, :], before[2][1], ALU.mult))
                own.step(TT(ex[:, 7, :], ex[:, 6, :], v_p, ALU.mult))
                own.wait()
                own.step(TT(ex[:, 0, :], ex[:, 0, :], ex[:, 1, :], ALU.add))
                own.step(TT(ex[:, 2, :], ex[:, 2, :], ex[:, 3, :], ALU.add))
                own.wait()
                own.step(TT(ex[:, 2, :], ex[:, 2, :], ex[:, 6, :], ALU.add))
                own.step(TT(ex[:, 0, :], ex[:, 0, :], ex[:, 7, :], ALU.add))
                own.wait()
                own.then(dve.reciprocal(ex[:, 2, :], ex[:, 2, :]))
                own.then(TT(ex[:, 0, :], ex[:, 0, :], ex[:, 2, :], ALU.mult))
                s_kvr.wait_taken(dve, 6 * p + 5)
                TT(sr[:, lo:hi], sr[:, lo:hi], ex[:, 0, :], ALU.mult).then_inc(ry_ready, 1)
            for i in range(NT):
                s_wo4.wait_filled(dve, i)
                TT(x1[:, i, :], x1[:, i, :], bank(s_wo4.banks[i][0], TILE, 0, D), ALU.add)\
                    .then_inc(s_wo4.taken["dve"], 1)
            for k in range(2):
                norm_stats(x1, k, lambda i: s_wo4.wait_taken(dve, i))
                for i in range(8 * k, 8 * k + 8):
                    normalise(xa, x1, i, rstd).then_inc(xb_ready, 1)
            for i in range(24):
                q, m = divmod(i, 6)
                s_kf.wait_taken(dve, i)
                TT(kf[:, m, quarter(q)], relu_b[:, i % 4, :], relu_b[:, i % 4, :], ALU.mult)\
                    .then_inc(kf_ready, 1)
            for i in range(NT):
                s_vf.wait_filled(dve, i)
                s_rf.wait_taken(dve, i)
                own.wait()
                own.then(TT(gate[:, i % 2, :], bank(s_vf.banks[i][0], TILE, 0, D), sig[:, i, :], ALU.mult))
                TT(x1[:, i, :], x1[:, i, :], gate[:, i % 2, :], ALU.add).then_inc(s_vf.taken["dve"], 1)

            twice_normed(h, x5, xb_, lambda i: dve.wait_ge(h_plus, i + 1), x5_ready)
            dve.wait_ge(const_ready, MIX_CONST + 2)

            def values(i):
                s_vb.wait_filled(dve, i)
                if i >= 4:
                    s_pv.wait_filled(dve, i - 4)
                vm = vmask.rearrange("p h d -> p (h d)").unsqueeze(1).broadcast_to([TILE, 2, D])
                TT(vblk[:, 2 * (i % 4):2 * (i % 4) + 2, :],
                   bank(s_vb.banks[i][0], TILE, 0, 2 * D).rearrange("p (j n) -> p j n", j=2), vm,
                   ALU.mult).then_inc(s_vb.taken["dve"], 1)

            def heads(v):
                return v.rearrange("p (b h) l -> p b h l", b=2)

            def less_max(i):
                s_sc.wait_filled(dve, i)
                ps = psum[1 + i % 2][0:PAIR, :].rearrange("p (b n) -> p b n", b=2)[:, :, 0:6 * TOKENS]\
                    .rearrange("p b (h l) -> p b h l", l=TOKENS)
                mx = smax[:, i % 2, :].rearrange("p (b h) -> p b h", b=2)
                own.then(dve.tensor_reduce(mx, ps, AX.X, ALU.max))
                if i >= 2:
                    s_pT.wait_filled(dve, i - 2)
                for b in range(2):
                    ins = TT(prob[:, i % 2, 6 * b:6 * b + 6, :], ps[:, b],
                             mx[:, b].unsqueeze(2).broadcast_to([PAIR, 6, TOKENS]), ALU.subtract)
                    if b == 0:
                        own.step(ins)
                ins.then_inc(s_sc.taken["dve"], 1)

            def sums(i):
                dve.wait_ge(sexp, i + 1)
                own.then(dve.tensor_reduce(ssum[:, i % 2, :], prob[:, i % 2], AX.X, ALU.add))
                own.then(dve.reciprocal(rsum[:, i % 2, :], ssum[:, i % 2, :]))

            def context(i):
                s_pv.wait_filled(dve, i)
                if i >= 2:
                    s_cx.wait_filled(dve, i - 2)
                TT(ctxv[:, i % 2, :].rearrange("p (h d) -> p h d", d=HD),
                   bank(s_pv.banks[i][0], PAIR, 0, D).rearrange("p (h d) -> p h d", d=HD),
                   rsum[:, i % 2, :].unsqueeze(2).broadcast_to([PAIR, HEADS, HD]), ALU.mult)\
                    .then_inc(s_pv.taken["dve"], 1)

            def add_out(s, i):
                s.wait_filled(dve, i)
                TT(x5[:, i, :], x5[:, i, :], bank(s.banks[i][0], TILE, 0, D), ALU.add)\
                    .then_inc(s.taken["dve"], 1)

            own.wait()
            for i in range(NT + 4):
                if i < NT:
                    values(i)
                    less_max(i)
                if 2 <= i < NT + 2:
                    context(i - 2)
                if 1 <= i <= NT:
                    sums(i - 1)
                if i >= 4:
                    add_out(s_ow, i - 4)
            dve.wait_ge(loaded["mlpw0"], 16 * 4)
            for i in range(NT):
                s_mT.wait_filled(dve, 2 * (i // TQ) + 1)
                own.step(TT(x5[:, i, :], x5[:, i, :], mlp2b[0], ALU.add))
            own.wait()
            for i in range(NT):
                add_out(s_m2[0], i)
            for k in range(2):
                norm_stats(x5, k, lambda i: s_m2[0].wait_taken(dve, i))
                for i in range(8 * k, 8 * k + 8):
                    normalise(xb_, x5, i, rstd).then_inc(xm_ready, 1)
            s_gl.wait_filled(dve, 0)
            dve.tensor_copy(glog.rearrange("p t e -> p (t e)"), bank(s_gl.banks[0][0], TILE, 0, NT * NX))\
                .then_inc(s_gl.taken["dve"], 1)
            own.step(dve.memset(grank, 0.0))
            s_gl.wait_taken(dve, 0)
            own.wait()
            for f in range(NX):
                first = glog[:, :, f:f + 1]
                if f < NX - 1:
                    own.step(TT(gcmp[:, :, f + 1:NX], first.broadcast_to([TILE, NT, NX - 1 - f]),
                                glog[:, :, f + 1:NX], ALU.is_ge))
                if f > 0:
                    own.step(TT(gcmp[:, :, 0:f], first.broadcast_to([TILE, NT, f]),
                                glog[:, :, 0:f], ALU.is_gt))
                own.step(dve.memset(gcmp[:, :, f:f + 1], 0.0))
                own.wait()
                own.then(TT(grank, grank, gcmp, ALU.add))
            own.then(TS(grank, grank, 1.5, None, ALU.is_lt))
            own.then(dve.tensor_reduce(gm, glog, AX.X, ALU.max))
            TT(comb, glog, gm.unsqueeze(2).broadcast_to([TILE, NT, NX]), ALU.subtract).then_inc(comb_sub, 1)
            dve.wait_ge(comb_exp, 1)
            own.then(TT(comb, comb, grank, ALU.mult))
            own.then(dve.tensor_reduce(gm, comb, AX.X, ALU.add))
            own.then(dve.reciprocal(gm, gm))
            own.then(TT(comb, comb, gm.unsqueeze(2).broadcast_to([TILE, NT, NX]), ALU.mult))
            for e in range(1, NX + 1):
                dve.wait_ge(loaded[f"mlpw{e % 2}"], 16 * 4 * (e // 2 + 1))
                for i in range(NT):
                    if e == 1:
                        dve.wait_ge(h_plus, NT + i + 1)
                    else:
                        s_m2[e - 1].wait_taken(dve, i)
                    own.step(STT(h[:, i, :], mlp2b[e % 2], comb[:, i, e - 1:e], h[:, i, :],
                                 ALU.mult, ALU.add))
                own.wait()
                for i in range(NT):
                    s_m2[e].wait_filled(dve, i)
                    STT(h[:, i, :], bank(s_m2[e].banks[i][0], TILE, 0, D), comb[:, i, e - 1:e],
                        h[:, i, :], ALU.mult, ALU.add).then_inc(s_m2[e].taken["dve"], 1)

        @block.tensor
        def _(pe):
            def mm(dst, lhsT, rhs, first, last):
                return pe.matmul(dst, lhsT, rhs, start=first, stop=last)

            def transposed(s, src, ready, parts=CH, chunk=lambda c: slice(c * CH, (c + 1) * CH)):
                for i in range(8):
                    q, c = divmod(i, 2)
                    s.fill(pe, i)
                    for t in range(TQ):
                        ready(4 * q + t)
                        ins = pe.transpose(bank(s.banks[i][0], parts, t * TILE, (t + 1) * TILE),
                                           src[:, 4 * q + t, chunk(c)], ident[0:TILE, 0:TILE])
                    ins.then_inc(s.filled, 1)

            def hidden_layer(s, w, src, rows, ready):
                for i in range(24):
                    q, m = divmod(i, 6)
                    if m == 0:
                        ready(q)
                    s.fill(pe, i)
                    for c in range(2):
                        k = rows[c]
                        ins = mm(bank(s.banks[i][0], 128, 0, QT), w[0:k, c, 128 * m:128 * m + 128],
                                 src[0:k, c, quarter(q)], c == 0, c == 1)
                    ins.then_inc(s.filled, 1)

            def output_layer(s, src, w, ready):
                for i in range(NT):
                    ready(i)
                    s.fill(pe, i)
                    dst = bank(s.banks[i][0], TILE, 0, D)
                    for m in range(HC):
                        ins = mm(dst, src[:, m, cols(i)], w[:, m, :], m == 0, m == HC - 1)
                    ins.then_inc(s.filled, 1)

            pe.wait_ge(loaded["tok_w"], 16)
            for i in range(NT):
                pe.wait_ge(loaded[f"p{i // TQ}"], 16)
                s_tok.fill(pe, i)
                for c in range(PATCH_CHUNKS):
                    ins = mm(bank(s_tok.banks[i][0], TILE, 0, D), patches[:, c, cols(i)], w_tok[:, c, :],
                             c == 0, c == PATCH_CHUNKS - 1)
                ins.then_inc(s_tok.filled, 1)
            pe.wait_ge(const_ready, 3)
            transposed(s_xhT, xh, lambda i: pe.wait_ge(xh_ready, i + 1))

            for r in range(2):
                pe.wait_ge(loaded[f"m{r}"], 16 * 9)
                for i in range(24):
                    q, m = divmod(i, 6)
                    s_xhT.wait_taken(pe, 2 * q + 1)
                    s_xz[r].fill(pe, i)
                    for c in range(2):
                        ins = mm(bank(s_xz[r].banks[i][0], 128, 0, QT), w_in[:, c, 128 * m:128 * m + 128],
                                 xhT[:, c, quarter(q)], c == 0, c == 1)
                    ins.then_inc(s_xz[r].filled, 1)
                for q in range(NQ):
                    pe.wait_ge(xconv_ready, r * 12 + 3 * q + 3)
                    s_xp[r].fill(pe, q)
                    for c in range(3):
                        ins = mm(bank(s_xp[r].banks[q][0], 108, 0, QT), w_x[:, c, :], gq(xconv, c, q),
                                 c == 0, c == 2)
                    ins.then_inc(s_xp[r].filled, 1)
                for i in range(12):
                    c, q = divmod(i, 4)
                    pe.wait_ge(dtr_ready, 4 * r + q + 1)
                    s_dt[r].fill(pe, i)
                    mm(bank(s_dt[r].banks[i][0], 128, 0, QT), w_dt[96:108, 128 * c:128 * c + 128],
                       dtr[96:108, quarter(q)], True, True).then_inc(s_dt[r].filled, 1)
                s_dt[r].wait_taken(pe, 11)
                pe.wait_ge(bc_ready, 4 * (r + 1))

                def spread(k, row, half, signal):
                    for lo, hi in ((0, 512), (512, HALF)):
                        ins = mm(psum[k // 2][:, lo:hi], sel[:, row, :],
                                 bc[:, half * HALF + lo:half * HALF + hi], True, True)
                    ins.then_inc(signal, 1)

                def add_state(n):
                    u, j = r * UNITS + n, n % NS
                    pe.wait_ge(times_c, u + 1)
                    g = n // NS
                    if j == 0 and y_bank(g) == 6:
                        pe.wait_ge(c_ready, (r * 2 + g // 3 + 1) * NS)
                    elif j == 0 and g > 0:
                        last = max(k for k in range(g) if y_bank(k) == 4)
                        pe.wait_ge(y_taken, r * GROUPS + last + 1)
                    for lo, hi in ((0, 512), (512, HALF)):
                        ins = mm(psum[y_bank(g) // 2][:, lo:hi], ident[:, :], hbuf[:, u % SLOTS, lo:hi], j == 0, j == NS - 1)
                    ins.then_inc(summed, 1)

                for n in range(UNITS + 3):
                    u = r * UNITS + n
                    if n < UNITS:
                        if u >= 2:
                            pe.wait_ge(times_b, u - 1)
                        spread(2 * (u % 2), n % NS, n // NS // 3, b_filled)
                        if n // NS % 3 == 0:
                            k = (r * 2 + n // NS // 3) * NS + n % NS
                            if k >= 1:
                                pe.wait_ge(c_ready, k)
                            if n == 3 * NS:
                                pe.wait_ge(y_taken, r * GROUPS + 2)
                            spread(6, NS + n % NS, n // NS // 3, c_filled)
                    if n >= 3:
                        add_state(n - 3)
                pe.wait_ge(c_ready, 2 * NS * (r + 1))
                pe.wait_ge(scanned, UNITS * (r + 1))
                pe.wait_ge(gated, GROUPS * (r + 1))
                pe.wait_ge(loaded[f"wout{r}"], 16)
                for i in range(NT):
                    s_wo[r].fill(pe, i)
                    t0 = i % 8 * TILE
                    for c in range(3):
                        ins = mm(bank(s_wo[r].banks[i][0], TILE, 0, D), zs[:, i // 8 * 3 + c, t0:t0 + TILE],
                                 w_out[r][:, c, :], c == 0, c == 2)
                    ins.then_inc(s_wo[r].filled, 1)

            pe.wait_ge(phi_ready, 1)
            for c in range(2):
                s_phi.fill(pe, c)
                pe.transpose(bank(s_phi.banks[c][0], CH, 0, NE), phiT[:, c::2], ident[0:NE, 0:NE])\
                    .then_inc(s_phi.filled, 1)
            transposed(s_xnT, xn, lambda i: pe.wait_ge(xn_ready, i + 1), chunk=lambda c: slice(c, D, 2))
            s_phi.wait_taken(pe, 1)
            for q in range(NQ):
                s_xnT.wait_taken(pe, 2 * q + 1)
                s_dl.fill(pe, q)
                for c in range(2):
                    ins = mm(bank(s_dl.banks[q][0], NE, 0, QT), phin[:, c, :], xnT[:, c, quarter(q)],
                             c == 0, c == 1)
                ins.then_inc(s_dl.filled, 1)
            for k in range(2):
                s_cl.fill(pe, k)
                for t in range(8):
                    for c in range(2):
                        ins = mm(bank(s_cl.banks[k][0], TILE, t * NE, (t + 1) * NE),
                                 xnT[:, c, cols(8 * k + t)], phin[:, c, :], c == 0, c == 1)
                ins.then_inc(s_cl.filled, 1)
            for i in range(NT):
                pe.wait_ge(dnorm, i // TQ + 1)
                s_dT.fill(pe, i)
                pe.transpose(bank(s_dT.banks[i][0], TILE, 0, NE),
                             dlog[:, 2 * i:2 * i + 2, :].rearrange("p i l -> p (i l)"),
                             ident[0:NE, 0:NE]).then_inc(s_dT.filled, 1)
            for i in range(NT):
                pe.wait_ge(cbd_ready, i + 1)
                s_cT.fill(pe, i)
                pe.transpose(bank(s_cT.banks[i][0], 128, 0, TILE), cbd[:, i % 2, :],
                             ident[0:TILE, 0:TILE]).then_inc(s_cT.filled, 1)
            for i in range(8):
                grp, c = divmod(i, 2)
                s_xs.fill(pe, i)
                for t in range(TQ):
                    s_dT.wait_taken(pe, 4 * grp + t)
                    ins = mm(bank(s_xs.banks[i][0], CH, t * 128, (t + 1) * 128),
                             xn[:, 4 * grp + t, c:D:2], dbd[:, 4 * grp + t, :], True, True)
                ins.then_inc(s_xs.filled, 1)
            s_xs.wait_taken(pe, 7)

            def expert_hidden(g):
                b = g % 2
                pe.wait_ge(loaded[f"w1e{b}"], 16 * 2 * (g // 2 + 1))
                for k in range(2):
                    i = 2 * g + k
                    s_h1.fill(pe, i)
                    for c in range(2):
                        rows = CH + c
                        for j in range(EG):
                            ins = mm(bank(s_h1.banks[i][0], 32 * j + 32, 0, QH, 32 * j),
                                     xsT[0:rows, c, EG * g + j, :],
                                     w1e[0:rows, b, 2 * j + c, k * QH:(k + 1) * QH], c == 0, c == 1)
                    ins.then_inc(s_h1.filled, 1)

            def expert_turn(g):
                for k in range(2):
                    i = 2 * g + k
                    s_h1.wait_taken(pe, 2 * g + 1)
                    s_hT.fill(pe, i)
                    for m in range(3):
                        ins = pe.transpose(bank(s_hT.banks[i][0], 128, 128 * m, 128 * m + 128),
                                           hid_e[:, g % 2, 3 * k + m:HID:HC], ident[:, :])
                    ins.then_inc(s_hT.filled, 1)

            def expert_output(g):
                b = g % 2
                s_y2.fill(pe, g)
                pe.wait_ge(loaded[f"w2e{b}"], 16 * 2 * (g // 2 + 1))
                s_hT.wait_taken(pe, 2 * g + 1)
                for j in range(EG):
                    mm(bank(s_y2.banks[g][0], 32 * j + 32, 0, D, 32 * j), ones[0:1, 0:32],
                       b2e[:, b, j * D:(j + 1) * D], True, False)
                for m in range(HC):
                    for j in range(EG):
                        ins = mm(bank(s_y2.banks[g][0], 32 * j + 32, 0, D, 32 * j),
                                 hidT[:, b, m, 32 * j:32 * j + 32], w2e[:, b, HC * j + m, :],
                                 False, m == HC - 1)
                ins.then_inc(s_y2.filled, 1)

            for g in range(NG + 2):
                if g < NG:
                    expert_hidden(g)
                if 1 <= g <= NG:
                    expert_turn(g - 1)
                if g >= 2:
                    expert_output(g - 2)
            for k in range(2):
                pe.wait_ge(ys_stored[k], 16 * 8 * NG // 2)
            for i in range(NT):
                s_cT.wait_taken(pe, i)
                s_mix.fill(pe, i)
                mm(bank(s_mix.banks[i][0], TILE, 0, D), cT[:, i, :], ysN[:, i, :], True, True)\
                    .then_inc(s_mix.filled, 1)

            transposed(s_xaT, xa, lambda i: pe.wait_ge(xa_ready, i + 1))
            pe.wait_ge(loaded["rw"], 16 * RW_LOADS)
            for i in range(18):
                w, p, part = KVR[i]
                s_kvr.fill(pe, i)
                if p < 2:
                    q = 2 * p + part
                    s_xaT.wait_taken(pe, 2 * q + 1)
                    for c in range(2):
                        ins = mm(bank(s_kvr.banks[i][0], 128, 0, QT), w_kvr[:, c, w * D:w * D + 128],
                                 xaT[:, c, quarter(q)], c == 0, c == 1)
                else:
                    for half in range(2):
                        for c in range(2):
                            ins = mm(bank(s_kvr.banks[i][0], 64 * half + 64, 0, QT, 64 * half),
                                     w_kvr[:, c, w * D + 128:w * D + D],
                                     xaT[:, c, quarter(2 * half + part)], c == 0, c == 1)
                ins.then_inc(s_kvr.filled, 1)
            pe.wait_ge(loaded["rwB"], 16 * 6)
            pe.wait_ge(ry_ready, 3)
            for i in range(NT):
                s_wo4.fill(pe, i)
                dst = bank(s_wo4.banks[i][0], TILE, 0, D)
                half = i // 8
                mm(dst, sr[:, i * TILE:(i + 1) * TILE], w_oA[:, :], True, False)
                at = T + i % 8 * TILE
                mm(dst, sr[64 * half:64 * half + 64, at:at + TILE], w_oB[64 * half:64 * half + 64, :],
                   False, True).then_inc(s_wo4.filled, 1)
            transposed(s_xbT, xa, lambda i: pe.wait_ge(xb_ready, i + 1))
            for i in range(NT):
                s_xbT.wait_taken(pe, 2 * (i // TQ) + 1)
                s_rf.fill(pe, i)
                for c in range(2):
                    ins = mm(bank(s_rf.banks[i][0], TILE, 0, D), xaT[:, c, cols(i)], w_rf[:, c, :],
                             c == 0, c == 1)
                ins.then_inc(s_rf.filled, 1)
            hidden_layer(s_kf, w_kf, xaT, (CH, CH), lambda q: None)
            output_layer(s_vf, kf, w_vf, lambda i: pe.wait_ge(kf_ready, 6 * (i // TQ) + 6))

            transposed(s_x5T, xb_, lambda i: pe.wait_ge(x5_ready, i + 1))
            pe.wait_ge(loaded["tb"], 16 * 10)
            pe.wait_ge(const_ready, MIX_CONST + 2)
            for i in range(16):
                q, which, c = i // 4, i // 2 % 2, i % 2
                s_x5T.wait_taken(pe, 2 * q + 1)
                s_qk.fill(pe, i)
                for k in range(2):
                    rows = CH + k
                    at = which * D + c * CH
                    ins = mm(bank(s_qk.banks[i][0], CH, 0, QT), in_w[0:rows, k, at:at + CH],
                             x5T[0:rows, k, quarter(q)], k == 0, k == 1)
                ins.then_inc(s_qk.filled, 1)

            def value_rows(i):
                s_vb.fill(pe, i)
                for j in range(2):
                    at = (2 * i + j) * TILE
                    for k in range(2):
                        rows = CH + k
                        ins = mm(bank(s_vb.banks[i][0], TILE, j * D, (j + 1) * D),
                                 x5two[0:rows, k, at:at + TILE],
                                 in_w[0:rows, k, 2 * D:3 * D], k == 0, k == 1)
                ins.then_inc(s_vb.filled, 1)

            def score_rows(i):
                s_sc.fill(pe, i)
                pe.wait_ge(kblk_ready, 4 * i + 4)
                for j in range(2):
                    at = (2 * i + j) * TOKENS
                    width = 64 if j == 0 else TOKENS
                    for c in range(2):
                        ins = mm(bank(2 + 2 * (i % 2) + c, 64 * j + width, 0, 6 * TOKENS, 64 * j),
                                 qT[:, c, at:at + width], kblk[:, 4 * (i % 2) + 2 * j + c, :], True, True)
                ins.then_inc(s_sc.filled, 1)

            def prob_turn(i):
                pe.wait_ge(sexp, i + 1)
                s_pT.fill(pe, i)
                for g in range(6):
                    ins = pe.transpose(bank(6 + g // 3, TILE, g % 3 * PAIR, (g % 3 + 1) * PAIR),
                                       prob[:, i % 2, 2 * g:2 * g + 2, :].rearrange("p h l -> p (h l)"),
                                       ident[0:PAIR, 0:PAIR])
                ins.then_inc(s_pT.filled, 1)

            def context_rows(i):
                s_pv.fill(pe, i)
                s_pT.wait_taken(pe, i)
                s_vb.wait_taken(pe, i)
                for j in range(2):
                    width = 64 if j == 0 else TOKENS
                    for g in range(6):
                        ins = mm(bank(s_pv.banks[i][0], 64 * j + width, 32 * g, 32 * g + 32, 64 * j),
                                 probT[:, 6 * (i % 4) + g, 64 * j:64 * j + width],
                                 vblk[:, 2 * (i % 4) + j, 32 * g:32 * g + 32], True, True)
                ins.then_inc(s_pv.filled, 1)

            def context_turn(i):
                s_cx.fill(pe, i)
                s_pv.wait_taken(pe, i)
                for c in range(2):
                    ins = pe.transpose(bank(s_cx.banks[i][0], CH, 128 * c, 128 * c + PAIR),
                                       ctxv[:, i % 2, c * CH:(c + 1) * CH], ident[0:PAIR, 0:PAIR])
                ins.then_inc(s_cx.filled, 1)

            def attention_out(i):
                s_ow.fill(pe, i)
                s_cx.wait_taken(pe, i)
                for k in range(2):
                    ins = mm(bank(s_ow.banks[i][0], TILE, 0, D), ctxT[0:CH + k, k, cols(i)],
                             o_w[0:CH + k, k, :], k == 0, k == 1)
                ins.then_inc(s_ow.filled, 1)

            for i in range(NT + 4):
                if i < NT:
                    value_rows(i)
                    score_rows(i)
                if 1 <= i <= NT:
                    prob_turn(i - 1)
                if 2 <= i < NT + 2:
                    context_rows(i - 2)
                if 3 <= i < NT + 3:
                    context_turn(i - 3)
                if i >= 4:
                    attention_out(i - 4)
            transposed(s_mT, x5, lambda i: s_ow.wait_taken(pe, i))

            def mlp(e, turned):
                b = e % 2
                pe.wait_ge(loaded[f"mlpw{b}"], 16 * 4 * (e // 2 + 1))
                hidden_layer(s_m1[e], mlp1[b], x5T, (CH, CH + 1),
                             lambda q: turned.wait_taken(pe, 2 * q + 1))
                output_layer(s_m2[e], hid[b], mlp2[b],
                             lambda i: s_m1[e].wait_taken(pe, 6 * (i // TQ) + 5))

            mlp(0, s_mT)
            transposed(s_xmT, xb_, lambda i: pe.wait_ge(xm_ready, i + 1))
            s_gl.fill(pe, 0)
            for i in range(NT):
                s_xmT.wait_taken(pe, 2 * (i // TQ) + 1)
                for k in range(2):
                    ins = mm(bank(s_gl.banks[0][0], TILE, NX * i, NX * i + NX), x5T[0:CH + k, k, cols(i)],
                             gate_w[0:CH + k, k, :], k == 0, k == 1)
            ins.then_inc(s_gl.filled, 1)
            for e in range(1, NX + 1):
                mlp(e, s_xmT)


def chunked(w, n):
    k, m = w.shape
    return w.reshape(n, k // n, m).transpose(1, 0, 2)


def laid_out(p):
    o = {}
    gh = 7
    x = p["x"].reshape(IMAGES, 3, gh, 16, gh, 16).transpose(1, 3, 5, 0, 2, 4).reshape(768, T)
    o["patches"] = chunked(x, PATCH_CHUNKS)
    o["tok_w"] = chunked(p["L0_tok_W"].T, PATCH_CHUNKS)
    for r in ("fwd", "bwd"):
        q = {k: p[f"L0_attn_{r}_{k}"] for k in
             ("W_in", "conv_w", "conv_b", "W_x", "W_dt", "b_dt", "A_log", "D", "W_out")}
        o[f"{r}_w_in"] = chunked(q["W_in"].T, 2)
        o[f"{r}_conv_w"] = chunked(q["conv_w"], 3)
        for k in ("conv_b", "b_dt", "D"):
            o[f"{r}_{k.lower()}"] = q[k].reshape(3, 128).T
        o[f"{r}_a_log"] = chunked(q["A_log"], 3).reshape(128, 3 * NS)
        o[f"{r}_w_bc"] = chunked(q["W_x"][RANK:].T, 3)
        o[f"{r}_w_dtr"] = chunked(q["W_x"][:RANK].T, 3)
        o[f"{r}_w_dt"] = q["W_dt"].T
        o[f"{r}_w_out"] = chunked(q["W_out"].T, 3)
    o["ln_g"], o["ln_b"] = p["L0_attn_ln_g"], p["L0_attn_ln_b"]
    o["phi"] = p["L0_ffn_phi"][:, :, 0].T
    o["scale"] = p["L0_ffn_scale"]
    for k in ("w1", "b1", "w2", "b2"):
        o[f"e_{k}"] = p[f"L0_ffn_{k}"]
    q = {k: p[f"L1_attn_{k}"] for k in ("ln1_w", "ln1_b", "ln2_w", "ln2_b", "decay", "first", "Wk_a",
                                        "Wv_a", "Wr_a", "Wo_a", "Wk_f", "Wv_f", "Wr_f")}
    o["w_kvr"] = chunked(np.concatenate([q["Wk_a"], q["Wv_a"], q["Wr_a"]]).T, 2)
    o["w_o"] = q["Wo_a"].T
    o["w_kf"], o["w_vf"], o["w_rf"] = chunked(q["Wk_f"].T, 2), chunked(q["Wv_f"].T, HC), chunked(q["Wr_f"].T, 2)
    for k in ("ln1_w", "ln1_b", "ln2_w", "ln2_b"):
        o[f"r_{k}"] = q[k].reshape(2, CH).T
    o["decay"], o["first"] = q["decay"].reshape(D, 1), q["first"].reshape(D, 1)
    q = {k: p[f"L1_ffn_{k}"] for k in
         ("ln1_g", "ln1_b", "in_w", "in_b", "out_w", "out_b", "mlp_w1", "mlp_b1", "mlp_w2", "mlp_b2",
          "ln2_g", "ln2_b", "gate_w", "gate_b", "exp_w1", "exp_b1", "exp_w2", "exp_b2")}
    for k in ("ln1_g", "ln1_b", "ln2_g", "ln2_b"):
        o[f"t_{k}"] = q[k].reshape(2, CH).T
    o["in_w"], o["in_b"] = chunked(q["in_w"].T, 2), q["in_b"].reshape(1, -1)
    o["out_w"], o["out_b"] = chunked(q["out_w"].T, 2), q["out_b"].reshape(1, -1)
    o["gate_w"], o["gate_b"] = chunked(q["gate_w"].T, 2), q["gate_b"].reshape(1, -1)
    for e in range(NX + 1):
        w1, b1, w2, b2 = ((q[f"mlp_{k}"] for k in ("w1", "b1", "w2", "b2")) if e == 0 else
                          (q[f"exp_{k}"][e - 1] for k in ("w1", "b1", "w2", "b2")))
        o[f"mlp_w1_{e}"], o[f"mlp_b1_{e}"] = chunked(w1, 2), b1.reshape(1, -1)
        o[f"mlp_w2_{e}"], o[f"mlp_b2_{e}"] = chunked(w2, HC), b2
    return {k: np.ascontiguousarray(v) for k, v in o.items()}


def kernel(**inputs):
    import concourse.bacc as bacc
    from concourse.bass_utils import run_bass_kernel_spmd

    arrays = laid_out({k: np.asarray(v) for k, v in inputs.items()})
    nc = bacc.Bacc("TRN2", target_bir_lowering=False, num_devices=1)
    aps = {k: nc.dram_tensor(f"in_{k}", v.shape, mybir.dt.from_np(v.dtype), kind="ExternalInput").ap()
           for k, v in arrays.items()}
    out = nc.dram_tensor("out", (TILE, NT, D), F32, kind="ExternalOutput").ap()
    build_tower(nc, aps, out)
    r = run_bass_kernel_spmd(nc, [{f"in_{k}": v for k, v in arrays.items()}], core_ids=[0])
    got = r.results[0]["out"]
    return np.ascontiguousarray(got.transpose(1, 0, 2)).reshape(IMAGES, TOKENS, D)
```
